# Optimizing a Trainium2 kernel written in Bass

```python
import numpy as np
import jax
import jax.numpy as jnp

def _softmax(x, axis=-1):
    return jax.nn.softmax(x, axis=axis)

def _gelu(x):
    return jax.nn.gelu(x, approximate=True)

def _silu(x):
    return jax.nn.silu(x)

def _sigmoid(x):
    return jax.nn.sigmoid(x)

def _layernorm(x, axis=-1, eps=1e-05):
    m = jnp.mean(x, axis=axis, keepdims=True)
    v = jnp.var(x, axis=axis, keepdims=True)
    return (x - m) / jnp.sqrt(v + eps)

def _scatter_add(tgt, idx, src, axis=0):
    return tgt.at[idx].add(src)

def _segment_sum(src, seg, n):
    return jax.ops.segment_sum(src, seg, n)
kernel_name = 'mk_seq_postln_d1_jaxref_r4_c45933'

def setup_inputs(seed: int=0):
    np.random.seed(seed)
    _w = jnp.asarray

    def _L0_attn_setup():
        import jax, jax.numpy as jnp
        import numpy as np
        K_FACTOR = 0.5
        key = jax.random.key(seed)
        k1, k2, k3, k4 = jax.random.split(key, 4)
        B, S, H, I = (1, 512, 1024, 2752)
        x = jax.random.normal(k1, (B, S, H), dtype=jnp.float32)
        w_gate = jax.random.normal(k2, (I, H), dtype=jnp.float32) * 0.02
        w_up = jax.random.normal(k3, (I, H), dtype=jnp.float32) * 0.02
        w_down = jax.random.normal(k4, (H, I), dtype=jnp.float32) * 0.02
        return {'x': x, 'w_gate': w_gate, 'w_up': w_up, 'w_down': w_down}
    _L0_attn_in = _L0_attn_setup()

    def _L0_ffn_setup():
        import jax, jax.numpy as jnp
        import numpy as np
        LORA_SCALING = 1.0 / 2.0

        def _qlora_linear(x, wq, A, B):
            w = jnp.tile(wq, (1, 4))
            base = x @ w.T
            lora = x @ A.T @ B.T
            return base + lora * LORA_SCALING
        key = jax.random.key(seed)
        ks = jax.random.split(key, 10)
        d, h, r = (1024, 2752, 2)
        return {'x': jax.random.normal(ks[0], (16, 1, d), dtype=jnp.float32), 'w1q': jax.random.normal(ks[1], (h, d // 4), dtype=jnp.float32) * 0.02, 'a1': jax.random.normal(ks[2], (r, d), dtype=jnp.float32) * 0.02, 'b1': jax.random.normal(ks[3], (h, r), dtype=jnp.float32) * 0.02, 'w3q': jax.random.normal(ks[4], (h, d // 4), dtype=jnp.float32) * 0.02, 'a3': jax.random.normal(ks[5], (r, d), dtype=jnp.float32) * 0.02, 'b3': jax.random.normal(ks[6], (h, r), dtype=jnp.float32) * 0.02, 'w2q': jax.random.normal(ks[7], (d, h // 4), dtype=jnp.float32) * 0.02, 'a2': jax.random.normal(ks[8], (r, h), dtype=jnp.float32) * 0.02, 'b2': jax.random.normal(ks[9], (d, r), dtype=jnp.float32) * 0.02}
    _L0_ffn_in = _L0_ffn_setup()
    _d = {'L0_attn_x': _L0_attn_in['x'], 'L0_attn_w_gate': _L0_attn_in['w_gate'], 'L0_attn_w_up': _L0_attn_in['w_up'], 'L0_attn_w_down': _L0_attn_in['w_down'], 'L0_ffn_w1q': _L0_ffn_in['w1q'], 'L0_ffn_a1': _L0_ffn_in['a1'], 'L0_ffn_b1': _L0_ffn_in['b1'], 'L0_ffn_w3q': _L0_ffn_in['w3q'], 'L0_ffn_a3': _L0_ffn_in['a3'], 'L0_ffn_b3': _L0_ffn_in['b3'], 'L0_ffn_w2q': _L0_ffn_in['w2q'], 'L0_ffn_a2': _L0_ffn_in['a2'], 'L0_ffn_b2': _L0_ffn_in['b2']}
    _x0 = _d['L0_attn_x']
    _d['L0_attn_x'] = jax.random.normal(jax.random.fold_in(jax.random.key(seed), 1), (2, 1024, 1024), dtype=_x0.dtype)
    del _x0
    return _d

def reference(L0_attn_x, L0_attn_w_gate, L0_attn_w_up, L0_attn_w_down, L0_ffn_w1q, L0_ffn_a1, L0_ffn_b1, L0_ffn_w3q, L0_ffn_a3, L0_ffn_b3, L0_ffn_w2q, L0_ffn_a2, L0_ffn_b2):

    def _L0_attn_ref(x, w_gate, w_up, w_down):
        import jax, jax.numpy as jnp
        import numpy as np
        K_FACTOR = 0.5
        s = jax.nn.silu(jnp.einsum('bsh,ih->bsi', x, w_gate))
        B, S, I = s.shape
        k = int(K_FACTOR * I)
        _, idx = jax.lax.top_k(-jnp.abs(s), k)
        flat = s.reshape(B * S, I)
        rows = jnp.arange(B * S)[:, None]
        flat = flat.at[rows, idx.reshape(B * S, k)].set(0.0)
        s = flat.reshape(B, S, I)
        s = s * jnp.einsum('bsh,ih->bsi', x, w_up)
        return jnp.einsum('bsi,hi->bsh', s, w_down)

    def _L0_ffn_ref(x, w1q, a1, b1, w3q, a3, b3, w2q, a2, b2):
        import jax, jax.numpy as jnp
        import numpy as np
        LORA_SCALING = 1.0 / 2.0

        def _qlora_linear(x, wq, A, B):
            w = jnp.tile(wq, (1, 4))
            base = x @ w.T
            lora = x @ A.T @ B.T
            return base + lora * LORA_SCALING
        gate = jax.nn.silu(_qlora_linear(x, w1q, a1, b1))
        up = _qlora_linear(x, w3q, a3, b3)
        return _qlora_linear(gate * up, w2q, a2, b2)
    x = L0_attn_x
    x = _layernorm(x + _L0_attn_ref(x, L0_attn_w_gate, L0_attn_w_up, L0_attn_w_down), axis=-1)
    x = _layernorm(x + _L0_ffn_ref(x, L0_ffn_w1q, L0_ffn_a1, L0_ffn_b1, L0_ffn_w3q, L0_ffn_a3, L0_ffn_b3, L0_ffn_w2q, L0_ffn_a2, L0_ffn_b2), axis=-1)
    return x

_drawn_inputs = setup_inputs


def setup_inputs(seed=0):
    import zlib

    import numpy as np

    out = dict(_drawn_inputs(seed))
    spreads = {}
    factors = {'L0_ffn_a1': 8.0,
     'L0_ffn_b1': 8.0,
     'L0_ffn_a3': 8.0,
     'L0_ffn_b3': 8.0,
     'L0_ffn_a2': 8.0,
     'L0_ffn_b2': 8.0}
    for name, (base, spread) in spreads.items():
        noise = np.random.default_rng([zlib.crc32(name.encode()), seed]).standard_normal(out[name].shape)
        drawn = base * np.exp(spread * noise) if base else spread * noise
        out[name] = jnp.asarray(drawn.astype(out[name].dtype))
    for name, factor in factors.items():
        out[name] = (out[name] * factor).astype(out[name].dtype)
    return out
```

```python
from contextlib import ExitStack

import concourse.bass as bass
from concourse import mybir

F32 = mybir.dt.float32
F32R = mybir.dt.float32r
I8 = mybir.dt.int8
I16 = mybir.dt.int16
I32 = mybir.dt.int32
ALU = mybir.AluOpType
ACT = mybir.ActivationFunctionType
AX = mybir.AxisListType
RMAX = bass.bass_isa.ReduceOp.max

P = 128
TOK, H, I = 2048, 1024, 2752
TB = 512
NB = TOK // TB
NT = TB // P
KH = H // P
CW = 344
NJ = I // CW
KEEP_FROM = I // 2
NC = -(-I // P)
LASTC = I - (NC - 1) * P
ROUNDS = 6
BIG = 1.0e30
EPS = 1e-5

NX, NG, ND, NU = KH, NJ * KH // 2, 2 * NC, NJ * KH // 2
RAW0 = NX + NG + NU
RAWB = NX + NG + ND + NU
USED0, USEDB = NG + NU, NG + ND + NU

Q4 = 4
HQ = H // Q4
KQ = HQ // P
IQ = I // Q4
CQ = -(-IQ // P)
LASTQ = IQ - (CQ - 1) * P
R = 2
LORA = 0.5
STEPS = CQ * Q4
LR = 96
RAW2 = RAW0 + RAWB * (NB - 1) + ND
NW2, NW13 = 2 * CQ, 4 * CQ
USED2 = USED0 + USEDB * (NB - 1) + ND


def rows_of(c):
    return P if c < CQ - 1 else LASTQ


class Steps:

    def __init__(self, eng, sem):
        self.eng, self.sem, self.base, self.n, self.outer = eng, sem, 0, 0, []

    def mark(self, ins):
        ins.then_inc(self.sem, 1)
        self.n += 1
        return self

    def done(self):
        self.eng.wait_ge(self.sem, self.base + self.n)

    def done_apart(self, passed):
        self.done()
        self.eng.sem_inc(passed, 1)

    def loop(self, i, per):
        self.outer.append((self.base, self.n))
        self.base, self.n = self.base + self.n + i * per, 0

    def end(self, per, count):
        assert self.n == per, (self.n, per)
        base, n = self.outer.pop()
        self.base, self.n = base, n + per * count


def program(nc, xT, xtok, wg, wu, wd, w13, w13t, w2, a13, a2, b1, b3, b2, out):
    x1 = nc.dram_tensor("x1", (NB, P, NT, H), F32, kind="Internal").ap()
    with ExitStack() as ctx:
        def sem(name):
            return ctx.enter_context(nc.semaphore(name))

        def bank(name):
            return ctx.enter_context(nc.psum_tensor(name, [P, 512], F32))

        room = 212600
        arena = ctx.enter_context(nc.sbuf_tensor("arena", [P, room], I8))
        start = nc.sbuf_base - room if nc.sbuf_base >= room else 0
        at = {"next": start}

        def sb(name, shape, dt, size, offset=None):
            n = size
            for d in shape[1:]:
                n *= d
            o = at["next"] if offset is None else offset
            if offset is None:
                at["next"] = -(-(o + n) // 32) * 32
                assert at["next"] <= start + room, (name, at["next"] - start)
            at[name] = o
            return nc.alloc_sbuf_tensor_at(name, shape, dt, offset=o)

        v = sb("v", [P, NT, I], F32, 4)
        hTh = sb("hTh", [P, NC, TB], F32R, 4)
        hTl = sb("hTl", [P, NC, TB], F32R, 4)
        xTh = sb("xTh", [P, KH, TB], F32R, 4)
        xTl = sb("xTl", [P, KH, TB], F32R, 4)
        raw = sb("raw", [P, 2, 2 * CW], F32, 4)
        wh = sb("wh", [P, 8 * CW], F32R, 4)
        wl = sb("wl", [P, 8 * CW], F32R, 4)
        sgn = sb("sgn", [P, NT, I], I8, 1)
        junkd = sb("junkd", [P, I], I8, 1)
        junka = sb("junka", [P, I // 2], I8, 1)
        ident = sb("ident", [P, P], F32, 4)
        y = sb("y", [P, NT, H], F32, 4, offset=at["hTh"])
        scr = sb("scr", [P, I // 4], F32, 4, offset=at["junkd"])
        mags = sb("mags", [P, NT, NJ], F32, 4)
        tc = sb("tc", [P, 2, NT], F32, 4)
        lc = sb("lc", [P, 2, NT], F32, 4)
        hc = sb("hc", [P, 2, NT], F32, 4)
        le = sb("le", [P, 2, NT], F32, 4)
        qa = sb("qa", [P, 2, NT], F32, 4)
        qb = sb("qb", [P, 2, NT], F32, 4)
        negt = sb("negt", [P, NT], F32, 4)
        ssum = sb("ssum", [P, 2, 2], F32, 4)
        sadd = sb("sadd", [P, 2], F32, 4)
        cand = sb("cand", [P, 32], F32, 4)
        top8 = sb("top8", [P, 8], F32, 4)
        pick = sb("pick", [P, 8], F32, 4)
        iota8 = sb("iota8", [P, 8], F32, 4)
        bad = sb("bad", [P, 1], F32, 4)
        flag = sb("flag", [P, 1], F32, 4)
        bit = sb("bit", [P, NT], I32, 4)
        taken = sb("taken", [P, NT], I32, 4)
        carry = sb("carry", [P, 1], F32, 4)
        stats = sb("stats", [P, NT, 2, 6], F32, 4)
        mv = sb("mv", [P, NT, 2], F32, 4)
        ve = sb("ve", [P, NT], F32, 4)
        mhalf = sb("mhalf", [P, NT], F32, 4)
        rstd = sb("rstd", [P, NT], F32, 4)
        nbias = sb("nbias", [P, NT], F32, 4)

        over = {"at": at["v"]}

        def put(name, shape, dt):
            n = 4
            for d in shape[1:]:
                n *= d
            o = over["at"]
            over["at"] = -(-(o + n) // 32) * 32
            return sb(name, shape, dt, 4, offset=o)

        w2h = put("w2h", [P, CQ, H], F32R)
        b13 = put("b13", [P, I], F32R)
        b2s = put("b2s", [P, H], F32R)
        a2s = put("a2s", [P, Q4, CQ, 2 * R], F32R)
        a2raw = put("a2raw", [P, Q4, CQ, R], F32)
        a13s = put("a13s", [P, KH, 2 * R], F32)
        keep = put("keep", [P, 2], F32)
        t2s = put("t2s", [P, TB], F32R)
        assert over["at"] <= at["hTh"]
        over["at"] = at["xTh"]
        w2l = put("w2l", [P, CQ, H], F32R)
        xa = put("xa", [P, 2, H], F32)
        assert over["at"] <= at["raw"]
        over["at"] = at["hTh"] + NT * H * 4
        w13h = put("w13h", [P, 8, 512], F32R)
        w13l = put("w13l", [P, 8, 512], F32R)
        x1T = put("x1T", [P, KH, P], F32)
        xf = put("xf", [P, KQ, P], F32)
        xsh = put("xsh", [P, KQ, TB], F32R)
        xsl = put("xsl", [P, KQ, TB], F32R)
        lg = put("lg", [P, TB], F32R)
        lu = put("lu", [P, TB], F32R)
        th = put("th", [P, TB], F32R)
        tl = put("tl", [P, TB], F32R)
        over_bt = over["at"]
        sg = put("sg", [P, 2, TB], F32)
        h2 = put("h2", [P, 2, TB], F32)
        h2h = put("h2h", [P, 2, TB], F32R)
        h2l = put("h2l", [P, 2, TB], F32R)
        fold = put("fold", [P, TB], F32)
        assert over["at"] <= at["xTh"]
        over["at"] = over_bt
        braw = put("braw", [P, I + H], F32)
        over["at"] = at["wh"]
        hqh = put("hqh", [P, CQ, TB], F32R)
        hql = put("hql", [P, CQ, TB], F32R)
        assert over["at"] <= at["junkd"]

        banks = [bank(f"bank{i}") for i in range(8)]

        raw_in = [sem(f"raw_in{i}") for i in range(2)]
        hi_done, lo_done, pe_used = sem("hi_done"), sem("lo_done"), sem("pe_used")
        g_done, g_freed = sem("g_done"), sem("g_freed")
        u_done, u_freed = sem("u_done"), sem("u_freed")
        t_done, t_hi, t_lo = sem("t_done"), sem("t_hi"), sem("t_lo")
        d_done, d_evac = sem("d_done"), sem("d_evac")
        probe, signs = sem("probe"), sem("signs")
        bad_ready, flag_ready = sem("bad_ready"), sem("flag_ready")
        x_in, ve_ready, rstd_ready, nb_ready, norm_done, x1_out = (
            sem("x_in"), sem("ve_ready"), sem("rstd_ready"), sem("nb_ready"), sem("norm_done"), sem("x1_out"))
        xa_in = [sem(f"xa_in{i}") for i in range(2)]
        small_in, b_zero, b_in, b_ready, a_ready, keep_ready = (
            sem("small_in"), sem("b_zero"), sem("b_in"), sem("b_ready"), sem("a_ready"), sem("keep_ready"))
        l_fold = sem("l_fold")
        x1t_done, x1t_ready, t1_done, l_ready = sem("x1t_done"), sem("x1t_ready"), sem("t1_done"), sem("l_ready")
        gg_done, uu_done, s_done, h_done, f_done = (
            sem("gg_done"), sem("uu_done"), sem("s_done"), sem("h_done"), sem("f_done"))
        hh_done, hl_done, t2_done, t2_ready = sem("hh_done"), sem("hl_done"), sem("t2_done"), sem("t2_ready")
        qh_done, ql_done, e_done, e_evac, y_in, out_done = (
            sem("qh_done"), sem("ql_done"), sem("e_done"), sem("e_evac"), sem("y_in"), sem("out_done"))
        passed_dve, passed_pool, passed_pe = sem("passed_dve"), sem("passed_pool"), sem("passed_pe")
        exact_s = sem("exact_s")
        consts, dve_s, act_s, pool_s = sem("consts"), sem("dve_s"), sem("act_s"), sem("pool_s")

        block = ctx.enter_context(nc.Block())

        def raw_base(b, first):
            return 0 if first else RAW0 + RAWB * (b - 1)

        def used_base(b, first):
            return 0 if first else USED0 + USEDB * (b - 1)

        def free_g(i, b, first):
            return (used_base(b, first) + i - 4 + 1) if (i >= 4 or not first) else None

        def free_d(i, base):
            return base - 4 + min(i, 2) + 1 if i < 4 else base + i - 4 + 1

        def free_u(i, base, first):
            if first or i >= 4:
                return base + i - 4 + 1
            return base - 4 + min(i + 1, 3) + 1

        @block.sync
        def _(sp):
            def load(n, slot, src, width):
                if n is not None:
                    sp.wait_ge(lo_done, n - 1)
                sp.dma_start(raw[0:src.shape[0], slot, 0:width], src).then_inc(raw_in[slot], 16)

            def load_x(b, base, first):
                for k in range(NX):
                    load(None if first and k < 2 else base + k, k % 2, xT[bass.ds(b, 1), :, k * TB:(k + 1) * TB]
                         .rearrange("o p n -> (o p) n"), TB)

            def load_gu(w, base):
                with sp.Fori(0, NJ // 2) as jj:
                    for i in range(8):
                        c = (i % 4) * 2 * CW
                        load(base + 8 * jj + i, i % 2,
                             w[bass.ds(2 * jj + i // 4, 1), :, c:c + 2 * CW].rearrange("o p n -> (o p) n"), 2 * CW)

            def load_d(base):
                with sp.Fori(0, NC - 1) as c:
                    for n in range(2):
                        load(base + 2 * c + n, n, wd[bass.ds(c * P, P), n * 512:(n + 1) * 512], 512)
                for n in range(2):
                    load(base + 2 * (NC - 1) + n, n, wd[(NC - 1) * P:I, n * 512:(n + 1) * 512], 512)

            def x_tiles(b1, used):
                sp.wait_ge(pe_used, used)
                sp.dma_start(y[:, :, :], xtok[bass.ds(b1, 1), :, :, :].rearrange("o p t h -> (o p) t h"))\
                    .then_inc(x_in, 16)

            load_x(0, 0, True)
            load_gu(wg, NX)
            load_gu(wu, NX + NG)
            with sp.Fori(1, NB) as b:
                base = raw_base(b, False)
                load_x(b, base, False)
                load_gu(wg, base + NX)
                load_d(base + NX + NG)
                x_tiles(b - 1, used_base(b, False) + NG + 16)
                load_gu(wu, base + NX + NG + ND)
            load_d(raw_base(NB, False))
            x_tiles(NB - 1, used_base(NB, False) + 16)
            for d in range(NW2):
                rows = rows_of(d // 2)
                load(RAW2 + d, d % 2, w2[d // 2 * P:d // 2 * P + rows, (d % 2) * 512:(d % 2 + 1) * 512], 512)
            sp.wait_ge(t_done, NC * NB)
            sp.dma_start(a13s[:, :, :], a13).then_inc(small_in, 16)
            for q in range(Q4):
                for c0, n in ((0, CQ - 1), (CQ - 1, 1)):
                    rows = rows_of(c0)
                    sp.dma_start(a2raw[0:rows, q, c0:c0 + n, :],
                                 a2[q * IQ + c0 * P:q * IQ + c0 * P + n * rows, :].rearrange("(c p) r -> p c r", p=rows))\
                        .then_inc(small_in, 16)
            sp.wait_ge(b_zero, 1)
            for g in range(3):
                for i, (src, c0) in enumerate(((b1, 0), (b3, 0), (b2, I), (b2, I))):
                    r0 = 32 * g + R * (i % 2)
                    sp.dma_start(braw[r0:r0 + R, c0:c0 + src.shape[1]], src).then_inc(b_in, 16)

            def load_xa(b):
                sp.wait_ge(x1_out, 16 * NT * (b + 1))
                for t in range(NT):
                    if t >= 2 or not (isinstance(b, int) and b == 0):
                        sp.wait_ge(x1t_done, NT * b + t - 1)
                    sp.dma_start(xa[:, t % 2, :], x1[bass.ds(b, 1), :, t, :].rearrange("o p h -> (o p) h"))\
                        .then_inc(xa_in[t % 2], 16)

            def load_13(b, chunks):
                base = RAW2 + NW2 + NW13 * b
                for c in chunks:
                    for i in range(4):
                        w, k = i // 2, i % 2
                        if c < CQ - 1:
                            load(base + 4 * c + i, i % 2, w13[c, w, k], 512)
                        else:
                            load(base + 4 * c + i, i % 2, w13t[w, k], Q4 * LASTQ)

            def load_y(b):
                sp.wait_ge(x1_out, 16 * NT * NB)
                if isinstance(b, int) and b == 0:
                    pass
                else:
                    sp.wait_ge(out_done, 16 * NT * b)
                sp.dma_start(y[:, :, :], x1[bass.ds(b, 1), :, :, :].rearrange("o p t h -> (o p) t h"))\
                    .then_inc(y_in, 16)

            load_13(0, (0,))
            load_xa(0)
            load_13(0, range(1, CQ))
            load_y(0)
            with sp.Fori(1, NB) as b:
                load_13(b, (0,))
                load_xa(b)
                load_13(b, range(1, CQ))
                load_y(b)
            sp.wait_ge(out_done, 16 * NT * NB)

        @block.gpsimd
        def _(pool):
            nc.gpsimd.memset(ident[:], 0.0).then_inc(pool_s, 1)
            pool.wait_ge(pool_s, 1)
            nc.gpsimd.affine_select(out=ident[:], in_=ident[:], compare_op=ALU.not_equal, fill=1.0, base=0,
                                    pattern=[[-1, P]], channel_multiplier=1).then_inc(consts, 1)
            nc.gpsimd.iota(iota8[:], pattern=[[1, 8]], base=0, channel_multiplier=0,
                           allow_small_or_imprecise_dtypes=True).then_inc(consts, 1)
            nc.gpsimd.memset(mhalf[:], -0.5).then_inc(pool_s, 1)
            pool.wait_ge(pool_s, 2)

            def low(n, slot, hi, lo, width, rows=P):
                pool.wait_ge(hi_done, n + 1)
                nc.gpsimd.tensor_tensor(lo, raw[0:rows, slot, 0:width], hi.bitcast(F32), ALU.subtract)\
                    .then_inc(lo_done, 1)

            def low_x(base):
                for k in range(NX):
                    low(base + k, k % 2, xTh[:, k, :], xTl[:, k, :], TB)

            def low_gu(base):
                with pool.Fori(0, NJ // 2) as jj:
                    for i in range(8):
                        s = slice((i % 4) * 2 * CW, (i % 4 + 1) * 2 * CW)
                        low(base + 8 * jj + i, i % 2, wh[:, s], wl[:, s], 2 * CW)

            def low_d(base):
                def one(n, d, rows):
                    s = slice((d % 4) * 512, (d % 4 + 1) * 512)
                    low(n, d % 2, wh[0:rows, s], wl[0:rows, s], 512, rows)
                with pool.Fori(0, NC // 2 - 1) as c:
                    for d in range(4):
                        one(base + 4 * c + d, d, P)
                for d in range(4):
                    one(base + ND - 4 + d, d, P if d < 2 else LASTC)

            def flagged(b):
                pool.wait_ge(bad_ready, b + 1)
                pool.sem_inc(passed_pool, 1)
                nc.gpsimd.partition_all_reduce(flag[:, 0:1], bad[:, 0:1], P, RMAX).then_inc(flag_ready, 1)

            def inv_std(b1):
                pool.wait_ge(ve_ready, b1 + 1)
                nc.gpsimd.tensor_tensor(rstd[:], ve[:], mhalf[:], ALU.pow).then_inc(rstd_ready, 1)

            low_x(0)
            low_gu(NX)
            flagged(0)
            low_gu(NX + NG)
            with pool.Fori(1, NB) as b:
                base = raw_base(b, False)
                low_x(base)
                low_gu(base + NX)
                low_d(base + NX + NG)
                flagged(b)
                inv_std(b - 1)
                low_gu(base + NX + NG + ND)
            low_d(raw_base(NB, False))
            for d in range(NW2):
                c, s, rows = d // 2, slice((d % 2) * 512, (d % 2 + 1) * 512), rows_of(d // 2)
                low(RAW2 + d, d % 2, w2h[0:rows, c, s], w2l[0:rows, c, s], 512, rows)
            inv_std(NB - 1)
            nc.gpsimd.memset(keep[:], 1.0).then_inc(pool_s, 1)
            pool.wait_ge(pool_s, 3)
            nc.gpsimd.affine_select(out=keep[:, 0:1], in_=keep[:, 0:1], compare_op=ALU.is_ge, fill=0.0, base=R - 1,
                                    pattern=[[0, 1]], channel_multiplier=-1).then_inc(keep_ready, 1)
            nc.gpsimd.affine_select(out=keep[:, 1:2], in_=keep[:, 1:2], compare_op=ALU.is_ge, fill=0.0, base=-R,
                                    pattern=[[0, 1]], channel_multiplier=1).then_inc(keep_ready, 1)
            pool.wait_ge(pe_used, USED2)
            nc.gpsimd.memset(braw[0:LR, :], 0.0).then_inc(b_zero, 1)
            for i, z in enumerate((lg, lu, t2s)):
                nc.gpsimd.memset(z[0:LR, :].bitcast(F32), 0.0).then_inc(keep_ready, 1)

            def low_13(b, c, i):
                s, m = (c % 2) * 4 + i, Q4 * rows_of(c)
                low(RAW2 + NW2 + NW13 * b + 4 * c + i, i % 2, w13h[:, s, 0:m], w13l[:, s, 0:m], m)

            def steps_2(b, last):
                def low_h(m):
                    rows = rows_of(m // Q4)
                    pool.wait_ge(hh_done, STEPS * b + m + 1)
                    nc.gpsimd.tensor_tensor(h2l[0:rows, m % 2, :], h2[0:rows, m % 2, :],
                                            h2h[0:rows, m % 2, :].bitcast(F32), ALU.subtract).then_inc(hl_done, 1)

                def low_q(c):
                    rows = rows_of(c)
                    pool.wait_ge(qh_done, CQ * b + c + 1)
                    nc.gpsimd.tensor_tensor(hql[0:rows, c, :], fold[0:rows, :], hqh[0:rows, c, :].bitcast(F32),
                                            ALU.subtract).then_inc(ql_done, 1)

                for m in range(STEPS):
                    c, q = m // Q4, m % Q4
                    if c < CQ - 1:
                        low_13(b, c + 1, q)
                    elif not last:
                        low_13(b + 1, 0, q)
                    if m:
                        low_h(m - 1)
                    if q == 0 and c:
                        low_q(c - 1)
                low_h(STEPS - 1)
                low_q(CQ - 1)

            for i in range(4):
                low_13(0, 0, i)
            with pool.Fori(0, NB - 1) as b:
                steps_2(b, False)
                inv_std(NB + b)
            steps_2(NB - 1, True)
            inv_std(2 * NB - 1)

        @block.scalar
        def _(act):
            st = Steps(act, act_s)

            def high(n, slot, hi, width, free, rows=P):
                act.wait_ge(raw_in[slot], n[0])
                if free is not None:
                    act.wait_ge(pe_used, free)
                nc.scalar.copy(hi, raw[0:rows, slot, 0:width]).then_inc(hi_done, 1)

            def landed(base, i):
                return [base * 8 + 16 * (i // 2) + 16]

            def high_x(base, b, first):
                for k in range(NX):
                    free = None if first else used_base(b, False) - 4 + k // 2 + 1
                    high(landed(base, k), k % 2, xTh[:, k, :], TB, free)

            def high_gu(base, jbase, i, free):
                s = slice((i % 4) * 2 * CW, (i % 4 + 1) * 2 * CW)
                high(landed(base, i + jbase * 0), i % 2, wh[:, s], 2 * CW, free)

            def high_d(base, d, used, rows=P):
                s = slice((d % 4) * 512, (d % 4 + 1) * 512)
                high(landed(base, d), d % 2, wh[0:(P if d < ND - 2 else LASTC), s], 512, free_d(d, used),
                     P if d < ND - 2 else LASTC)

            def evac(b, j, p, ubase):
                for t in range(NT):
                    if t < NT - 1:
                        act.wait_ge(g_done, 3 * NJ * b + 3 * j + t + 1)
                    else:
                        act.wait_ge(pe_used, ubase + 4 * j + 4)
                    nc.scalar.activation(v[:, t, bass.ds(j * CW, CW)], banks[4 * p + t][:, 0:CW], ACT.Silu)\
                        .then_inc(g_freed, 1)

            def gate(b, base, ubase, first):
                for i in range(4):
                    high(landed(base, i), i % 2, wh[:, i * 2 * CW:(i + 1) * 2 * CW], 2 * CW,
                         None if first else ubase - 4 + i + 1)
                if not first:
                    act.wait_ge(t_done, NC * b)

                def ahead(jj, q):
                    for i in range(4):
                        n = 4 * (q + 1) + i
                        high([base * 8 + 64 * jj + 16 * (n // 2) + 16], i % 2,
                             wh[:, i * 2 * CW:(i + 1) * 2 * CW], 2 * CW, ubase + 8 * jj + n - 4 + 1)

                with act.Fori(0, NJ // 2 - 1) as jj:
                    for q in range(2):
                        ahead(jj, q)
                        evac(b, 2 * jj + q, q, ubase)
                ahead(NJ // 2 - 1, 0)
                evac(b, NJ - 2, 0, ubase)
                return lambda: evac(b, NJ - 1, 1, ubase)

            def search(b, pieces):
                for r in range(ROUNDS):
                    act.wait_ge(probe, ROUNDS * b + r + 1)
                    for t in (2, 3):
                        for h in range(2):
                            st.done()
                            ins = nc.scalar.activation(junka[:, :], v[:, t, h * (I // 2):(h + 1) * (I // 2)], ACT.Sign,
                                                       bias=negt[:, t:t + 1], accum_out=ssum[:, t - 2, h:h + 1])
                            st.mark(ins)
                    st.done()
                    act.sem_inc(signs, 1)
                    pieces(r)

            def up(base, ubase, first, lead):
                for i in range(4):
                    if i >= lead:
                        high(landed(base, i), i % 2, wh[:, i * 2 * CW:(i + 1) * 2 * CW], 2 * CW,
                             free_u(i, ubase, first))
                for i in range(4, 8):
                    high(landed(base, i), i % 2, wh[:, (i - 4) * 2 * CW:(i - 3) * 2 * CW], 2 * CW, ubase + i - 3)
                with act.Fori(1, NJ // 2) as jj:
                    for i in range(8):
                        high([base * 8 + 64 * jj + 16 * (i // 2) + 16], i % 2,
                             wh[:, (i % 4) * 2 * CW:(i % 4 + 1) * 2 * CW], 2 * CW, ubase + 8 * jj + i - 3)

            def turned(b):
                for c in range(NC):
                    rows = P if c < NC - 1 else LASTC
                    act.wait_ge(t_done, NC * b + c + 1)
                    if c == 0:
                        act.wait_ge(x1_out, 16 * NT * b)
                    nc.scalar.copy(hTh[0:rows, c, :], banks[c % 8][0:rows, :]).then_inc(t_hi, 1)

            def norm(b1, n, dst, sent):
                act.wait_ge(nb_ready, n + 1)
                for t in range(NT):
                    nc.scalar.activation(y[:, t, :], y[:, t, :], ACT.Identity, scale=rstd[:, t:t + 1],
                                         bias=nbias[:, t:t + 1]).then_inc(norm_done, 1)
                for t in range(NT):
                    act.wait_ge(norm_done, NT * n + t + 1)
                    act.dma_start(dst[bass.ds(b1, 1), :, t, :].rearrange("o p h -> (o p) h"), y[:, t, :])\
                        .then_inc(sent, 16)

            high_x(0, 0, True)
            tail = gate(0, NX, 0, True)
            tail()
            search(0, lambda r: None)
            up(NX + NG, NG, True, 0)
            turned(0)
            with act.Fori(1, NB) as b:
                base, used = raw_base(b, False), used_base(b, False)
                st.loop(b - 1, 4 * ROUNDS)
                high_x(base, b, False)
                tail = gate(b, base + NX, used, False)
                dbase = base + NX + NG
                for d in range(4):
                    high_d(dbase, d, used + NG)
                tail()
                given = [4]

                def pieces(r):
                    for _ in range(5):
                        high_d(dbase, given[0], used + NG)
                        given[0] += 1

                search(b, pieces)
                while given[0] < ND:
                    high_d(dbase, given[0], used + NG)
                    given[0] += 1
                up(base + NX + NG + ND, used + NG + ND, False, 0)
                norm(b - 1, b - 1, x1, x1_out)
                turned(b)
                st.end(4 * ROUNDS, NB - 1)
            for d in range(ND):
                high_d(raw_base(NB, False), d, used_base(NB, False))
            for d in range(NW2):
                c, s, rows = d // 2, slice((d % 2) * 512, (d % 2 + 1) * 512), rows_of(d // 2)
                if d == 0:
                    act.wait_ge(t_done, NC * NB)
                high([RAW2 * 8 + 16 * (d // 2) + 16], d % 2, w2h[0:rows, c, s], 512, None, rows)
            norm(NB - 1, NB - 1, x1, x1_out)

            def high_13(b, c, i):
                s, m = (c % 2) * 4 + i, Q4 * rows_of(c)
                n = NW2 + NW13 * b + 4 * c + i
                if isinstance(b, int) and b == 0 and c < 2:
                    free = USED2
                else:
                    free = USED2 + NW13 * b + 4 * (c - 1)
                high([RAW2 * 8 + (NW2 + NW13 * b + 4 * c) * 8 + 16 * (i // 2) + 16], i % 2, w13h[:, s, 0:m], m, free)

            def turned_x(b, t):
                act.wait_ge(x1t_done, NT * b + t + 1)
                if not (isinstance(b, int) and b == 0 and t == 0):
                    act.wait_ge(t1_done, NT * b + t)
                    act.wait_ge(l_fold, NT * b + t)
                for i in range(2):
                    nc.scalar.copy(x1T[:, 4 * i:4 * i + 4, :].rearrange("p k t -> p (k t)"), banks[5 + i][:, :])\
                        .then_inc(x1t_ready, 1)

            def steps_2(b, last):
                def high_h(m):
                    rows = rows_of(m // Q4)
                    act.wait_ge(h_done, STEPS * b + m + 1)
                    if m >= 2:
                        act.wait_ge(t2_done, STEPS * b + m - 1)
                    nc.scalar.copy(h2h[0:rows, m % 2, :], h2[0:rows, m % 2, :]).then_inc(hh_done, 1)

                def high_q(c):
                    rows = rows_of(c)
                    act.wait_ge(f_done, CQ * b + c + 1)
                    nc.scalar.copy(hqh[0:rows, c, :], fold[0:rows, :]).then_inc(qh_done, 1)

                for m in range(STEPS):
                    c, q = m // Q4, m % Q4
                    if c < CQ - 1:
                        high_13(b, c + 1, q)
                    elif not last:
                        high_13(b + 1, 0, q)
                    rows = rows_of(c)
                    act.wait_ge(gg_done, STEPS * b + m + 1)
                    if m >= 2:
                        act.wait_ge(h_done, STEPS * b + m - 1)
                    nc.scalar.activation(sg[0:rows, m % 2, :], banks[2 * (m % 2)][0:rows, :], ACT.Silu).then_inc(s_done, 1)
                    if m:
                        high_h(m - 1)
                    if q == 0 and c:
                        high_q(c - 1)
                high_h(STEPS - 1)
                high_q(CQ - 1)

            for i in range(4):
                high_13(0, 0, i)
            for t in range(NT):
                turned_x(0, t)
            act.wait_ge(b_in, 16 * 12)
            nc.scalar.mul(b13[0:LR, :], braw[0:LR, 0:I], LORA).then_inc(b_ready, 1)
            nc.scalar.mul(b2s[0:LR, :], braw[0:LR, I:I + H], LORA).then_inc(b_ready, 1)
            with act.Fori(0, NB - 1) as b:
                steps_2(b, False)
                for t in range(NT):
                    turned_x(b + 1, t)
                norm(b, NB + b, out, out_done)
            steps_2(NB - 1, True)
            norm(NB - 1, 2 * NB - 1, out, out_done)

        @block.vector
        def _(dve):
            st = Steps(dve, dve_s)
            es = Steps(dve, exact_s)
            EXACT = 2 + 31 * (5 + NT) + NT + 1 + NT * (1 + 7 * NJ)
            V = nc.vector
            dve.sem_inc(g_freed, 8)
            dve.sem_inc(u_freed, 8)
            dve.wait_ge(consts, 2)

            def step(ins):
                st.mark(ins)

            def take_gate(b):
                with dve.Fori(0, NJ // 2) as jj:
                    st.loop(jj, 16)
                    for q in range(2):
                        for t in range(NT):
                            dve.wait_ge(g_freed, 8 + 4 * NJ * b + 8 * jj + 4 * q + t + 1)
                            s = v[:, t, bass.ds((2 * jj + q) * CW, CW)]
                            step(V.tensor_scalar(sgn[:, t, bass.ds((2 * jj + q) * CW, CW)], s, 0.0, 2.0,
                                                 ALU.is_ge, ALU.mult))
                            st.done()
                            step(V.scalar_tensor_tensor(out=s, in0=s, scalar=-1.0, in1=s, op0=ALU.mult, op1=ALU.max,
                                                        accum_out=mags[:, t, bass.ds(2 * jj + q, 1)]))
                    st.end(16, NJ // 2)

            def say_probe():
                st.done()
                V.tensor_scalar(negt[:], tc[:, 0, :], -1.0, None, ALU.mult).then_inc(probe, 1)

            def count(b, r):
                say_probe()
                for t in (0, 1):
                    step(V.tensor_scalar(junkd[:, :], v[:, t, :], tc[:, 0, t:t + 1], None, ALU.is_lt, ALU.add,
                                         accum_out=tc[:, 1, t:t + 1]))
                    st.done()
                dve.wait_ge(signs, ROUNDS * b + r + 1)
                step(V.tensor_tensor(sadd[:], ssum[:, :, 0], ssum[:, :, 1], ALU.add))
                st.done()
                step(V.tensor_scalar(sadd[:], sadd[:], -0.5, I / 2 - 0.25, ALU.mult, ALU.add))
                st.done()
                step(V.tensor_scalar(tc[:, 1, 2:4], sadd[:], 12582912.0, -12582912.0, ALU.add, ALU.add))
                st.done()

            def search(b):
                st.done()
                step(V.tensor_reduce(le[:, 0, :], mags[:], AX.X, ALU.add))
                st.done()
                step(V.tensor_scalar(tc[:, 0, :], le[:, 0, :], 0.75 / I, None, ALU.mult))
                step(V.memset(lc[:], 0.0))
                step(V.tensor_scalar(hc[:, 0, :], le[:, 0, :], 2.001 / I, None, ALU.mult))
                step(V.memset(hc[:, 1, :], float(I)))
                for r in range(ROUNDS):
                    count(b, r)
                    step(V.tensor_scalar(le[:], tc[:, 1:2, :].broadcast_to((P, 2, NT)), KEEP_FROM + 0.5, None, ALU.is_le))
                    st.done()
                    step(V.scalar_tensor_tensor(out=qa[:], in0=le[:], scalar=BIG, in1=tc[:], op0=ALU.mult, op1=ALU.max))
                    step(V.scalar_tensor_tensor(out=qb[:], in0=le[:], scalar=BIG, in1=tc[:], op0=ALU.mult, op1=ALU.min))
                    st.done()
                    step(V.tensor_tensor(hc[:], hc[:], qa[:], ALU.min))
                    step(V.tensor_tensor(lc[:], lc[:], qb[:], ALU.max))
                    st.done()
                    if r == ROUNDS - 1:
                        break
                    step(V.tensor_tensor(qa[:], hc[:], lc[:], ALU.subtract))
                    step(V.tensor_scalar(qb[:, 0, :], lc[:, 1, :], -1.0, KEEP_FROM + 4.0, ALU.mult, ALU.add))
                    st.done()
                    step(V.reciprocal(qb[:, 1, :], qa[:, 1, :]))
                    step(V.tensor_tensor(qa[:, 0, :], qa[:, 0, :], qb[:, 0, :], ALU.mult))
                    st.done()
                    step(V.tensor_tensor(qa[:, 0, :], qa[:, 0, :], qb[:, 1, :], ALU.mult))
                    st.done()
                    step(V.tensor_tensor(tc[:, 0, :], qa[:, 0, :], lc[:, 0, :], ALU.add))
                step(V.tensor_scalar(qa[:, 0, :], hc[:, 1, :], -(KEEP_FROM + 1.0), None, ALU.add))
                Q = I // 4
                for t in range(NT):
                    for c in range(4):
                        st.done()
                        step(V.scalar_tensor_tensor(out=scr[:], in0=v[:, t, c * Q:(c + 1) * Q], scalar=hc[:, 0, t:t + 1],
                                                    in1=v[:, t, c * Q:(c + 1) * Q], op0=ALU.is_lt, op1=ALU.mult))
                        st.done_apart(passed_dve)
                        step(V.max(out=cand[:, 8 * c:8 * c + 8], in_=scr[:]))
                    st.done_apart(passed_dve)
                    step(V.max(out=top8[:], in_=cand[:]))
                    st.done()
                    step(V.scalar_tensor_tensor(out=pick[:], in0=iota8[:], scalar=qa[:, 0, t:t + 1], in1=top8[:],
                                                op0=ALU.is_equal, op1=ALU.mult, accum_out=tc[:, 0, t:t + 1]))
                    st.done()
                    step(V.tensor_scalar(junkd[:, :], v[:, t, :], tc[:, 0, t:t + 1], None, ALU.is_lt, ALU.add,
                                         accum_out=tc[:, 1, t:t + 1]))
                st.done()
                step(V.tensor_scalar(le[:, 0, :], tc[:, 1, :], float(KEEP_FROM), None, ALU.not_equal))
                st.done()
                V.tensor_reduce(bad[:], le[:, 0, :], AX.X, ALU.max).then_inc(bad_ready, 1)
                dve.wait_ge(flag_ready, b + 1)
                dve.sem_inc(passed_dve, 1)
                flagged = dve.value_load(flag[0:1, 0:1].bitcast(I32))
                with dve.If(flagged != 0):
                    exact()
                with dve.Else():
                    dve.sem_inc(exact_s, EXACT)

            def exact():
                found, trial = tc[:, 0, :].bitcast(I32), le[:, 0, :].bitcast(I32)
                es.mark(V.memset(found, 0))
                es.mark(V.memset(bit[:], 1 << 30))
                with dve.Fori(0, 31) as i:
                    es.loop(i, 5 + NT)
                    es.done()
                    es.mark(V.tensor_tensor(trial, found, bit[:], ALU.bitwise_or))
                    es.done()
                    for t in range(NT):
                        es.mark(V.tensor_scalar(junkd[:, :], v[:, t, :], le[:, 0, t:t + 1], None, ALU.is_lt, ALU.add,
                                                accum_out=tc[:, 1, t:t + 1]))
                        es.done()
                    es.mark(V.tensor_scalar(taken[:], tc[:, 1, :], KEEP_FROM - 0.5, None, ALU.is_lt))
                    es.done()
                    es.mark(V.tensor_tensor(taken[:], taken[:], bit[:], ALU.mult))
                    es.done()
                    es.mark(V.tensor_tensor(found, found, taken[:], ALU.bitwise_or))
                    es.mark(V.tensor_scalar(bit[:], bit[:], 1, None, ALU.logical_shift_right))
                    es.end(5 + NT, 31)
                es.done()
                for t in range(NT):
                    es.mark(V.tensor_scalar(junkd[:, :], v[:, t, :], tc[:, 0, t:t + 1], None, ALU.is_lt, ALU.add,
                                            accum_out=tc[:, 1, t:t + 1]))
                    es.done()
                es.mark(V.tensor_scalar(qa[:, 0, :], tc[:, 1, :], -1.0, float(KEEP_FROM), ALU.mult, ALU.add))
                eq, nth = scr[:, 0:CW], scr[:, CW:2 * CW]
                for t in range(NT):
                    es.mark(V.memset(carry[:], 0.0))
                    with dve.Fori(0, NJ) as j:
                        es.loop(j, 7)
                        es.done()
                        g = sgn[:, t, bass.ds(j * CW, CW)]
                        es.mark(V.tensor_scalar(eq, v[:, t, bass.ds(j * CW, CW)], tc[:, 0, t:t + 1], None, ALU.is_equal))
                        es.done()
                        es.mark(V.tensor_tensor_scan(nth, eq, eq, carry[:, 0:1], ALU.add, ALU.max))
                        es.done()
                        es.mark(V.tensor_copy(carry[:], nth[:, CW - 1:CW]))
                        es.mark(V.scalar_tensor_tensor(out=eq, in0=nth, scalar=qa[:, 0, t:t + 1], in1=eq, op0=ALU.is_le,
                                                       op1=ALU.mult))
                        es.done()
                        es.mark(V.tensor_scalar(eq, eq, -1.0, 1.0, ALU.mult, ALU.add))
                        es.done()
                        es.mark(V.scalar_tensor_tensor(out=g, in0=g, scalar=-1.0, in1=eq, op0=ALU.add, op1=ALU.mult))
                        es.done()
                        es.mark(V.tensor_scalar(g, g, 1.0, None, ALU.add))
                        es.end(7, NJ)
                es.done_apart(passed_dve)
                assert es.n == EXACT

            def take_down(b1, used):
                dve.wait_ge(x_in, 16 * (b1 + 1))
                for n in range(2):
                    for t in range(NT):
                        if t < NT - 1:
                            dve.wait_ge(d_done, 6 * b1 + 3 * n + t + 1)
                        else:
                            dve.wait_ge(pe_used, used + ND - 1 + n)
                        s = y[:, t, n * 512:(n + 1) * 512]
                        V.tensor_tensor(s, banks[2 * t + n][:, :], s, ALU.add).then_inc(d_evac, 1)
                dve.wait_ge(d_evac, 8 * (b1 + 1))
                norm_sums(b1, None)

            def norm_sums(n, ready):
                for t in range(NT):
                    for i in range(2):
                        step(V.bn_stats(stats[:, t, i, :], y[:, t, i * 512:(i + 1) * 512]))
                    st.done_apart(passed_dve)
                    step(V.bn_aggr(mv[:, t, :], stats[:, t, :, :].rearrange("p n s -> p (n s)")))
                st.done()
                V.tensor_scalar(ve[:], mv[:, :, 1], EPS, None, ALU.add).then_inc(ve_ready, 1)
                dve.wait_ge(rstd_ready, n + 1)
                V.scalar_tensor_tensor(out=nbias[:], in0=mv[:, :, 0], scalar=-1.0, in1=rstd[:], op0=ALU.mult,
                                       op1=ALU.mult).then_inc(nb_ready, 1)

            def take_up(b, used):
                with dve.Fori(0, NJ // 2) as jj:
                    st.loop(jj, 16)
                    for q in range(2):
                        for t in range(NT):
                            j = 2 * jj + q
                            s, g = v[:, t, bass.ds(j * CW, CW)], sgn[:, t, bass.ds(j * CW, CW)]
                            st.done()
                            step(V.scalar_tensor_tensor(out=s, in0=s, scalar=tc[:, 0, t:t + 1], in1=s, op0=ALU.is_ge,
                                                        op1=ALU.mult))
                            st.done()
                            step(V.scalar_tensor_tensor(out=s, in0=g, scalar=-1.0, in1=s, op0=ALU.add, op1=ALU.mult))
                            st.done()
                            if t < NT - 1:
                                dve.wait_ge(u_done, 3 * NJ * b + 6 * jj + 3 * q + t + 1)
                            else:
                                dve.wait_ge(pe_used, used + 8 * jj + 4 * q + 4)
                            V.tensor_tensor(s, banks[4 * q + t][:, 0:CW], s, ALU.mult).then_inc(u_freed, 1)
                    st.end(16, NJ // 2)

            def turned(b):
                for c in range(NC):
                    rows = P if c < NC - 1 else LASTC
                    dve.wait_ge(t_hi, NC * b + c + 1)
                    V.tensor_tensor(hTl[0:rows, c, :], banks[c % 8][0:rows, :], hTh[0:rows, c, :].bitcast(F32),
                                    ALU.subtract).then_inc(t_lo, 1)

            def one(b):
                take_gate(b)
                search(b)

            n0 = st.n
            one(0)
            es.base, es.n = EXACT, 0
            take_up(0, NG)
            turned(0)
            per = st.n - n0 + 3 * NT
            with dve.Fori(1, NB) as b:
                st.loop(b - 1, per)
                es.loop(b - 1, EXACT)
                one(b)
                es.end(EXACT, NB - 1)
                used = used_base(b, False)
                take_down(b - 1, used + NG)
                take_up(b, used + NG + ND)
                turned(b)
                st.end(per, NB - 1)
            take_down(NB - 1, used_base(NB, False))
            dve.wait_ge(small_in, 16 * 9)
            A2 = [(slice(0, P), slice(0, CQ - 1)), (slice(0, LASTQ), slice(CQ - 1, CQ))]
            for p_, c_ in A2:
                step(V.tensor_copy(a2s[p_, :, c_, 0:R], a2raw[p_, :, c_, :]))
            st.done()
            for p_, c_ in A2:
                for q in range(Q4):
                    V.tensor_tensor(a2s[p_, q, c_, R:2 * R], a2raw[p_, q, c_, :], a2s[p_, q, c_, 0:R].bitcast(F32),
                                    ALU.subtract).then_inc(a_ready, 1)
            def fold_x(b, t):
                dve.wait_ge(x1t_ready, 2 * (NT * b + t + 1))
                if t == 0 and not (isinstance(b, int) and b == 0):
                    dve.wait_ge(uu_done, STEPS * b)
                st.done()
                V.tensor_reduce(xf[:], x1T[:, :, :].rearrange("p (q h) t -> p h t q", q=Q4), AX.X, ALU.add)\
                    .then_inc(l_fold, 1)
                dve.wait_ge(l_fold, NT * b + t + 1)
                tt = slice(t * P, (t + 1) * P)
                step(V.tensor_copy(xsh[:, :, tt], xf[:]))
                st.done()
                step(V.tensor_tensor(xsl[:, :, tt], xf[:], xsh[:, :, tt].bitcast(F32), ALU.subtract))

            def low_rank_x(b):
                dve.wait_ge(t1_done, NT * (b + 1))
                n = 2 * R
                step(V.tensor_copy(th[0:n, :], banks[7][0:n, :]))
                st.done()
                step(V.tensor_tensor(tl[0:n, :], banks[7][0:n, :], th[0:n, :].bitcast(F32), ALU.subtract))
                st.done()
                for i, dst in enumerate((lg, lu)):
                    for p0, src in ((0, th), (32, tl), (64, th)):
                        step(V.tensor_scalar(dst[p0:p0 + n, :], src[0:n, :].bitcast(F32), keep[0:n, i:i + 1], None,
                                             ALU.mult))
                st.done()
                dve.sem_inc(l_ready, 1)

            def steps_2(b):
                for m in range(STEPS):
                    c, q = m // Q4, m % Q4
                    rows = rows_of(c)
                    dve.wait_ge(uu_done, STEPS * b + m + 1)
                    dve.wait_ge(s_done, STEPS * b + m + 1)
                    if m >= 2:
                        dve.wait_ge(hl_done, STEPS * b + m - 1)
                    st.done()
                    V.tensor_tensor(h2[0:rows, m % 2, :], banks[2 * (m % 2) + 1][0:rows, :], sg[0:rows, m % 2, :],
                                    ALU.mult).then_inc(h_done, 1)
                    dve.wait_ge(h_done, STEPS * b + m + 1)
                    if q == 1:
                        if c:
                            dve.wait_ge(ql_done, CQ * b + c)
                        step(V.tensor_tensor(fold[0:rows, :], h2[0:rows, 0, :], h2[0:rows, 1, :], ALU.add))
                    elif q > 1:
                        st.done()
                        ins = V.tensor_tensor(fold[0:rows, :], fold[0:rows, :], h2[0:rows, m % 2, :], ALU.add)
                        if q == 3:
                            ins.then_inc(f_done, 1)
                            dve.wait_ge(f_done, CQ * b + c + 1)
                        else:
                            step(ins)

            def low_rank_h(b):
                n = 2 * R
                dve.wait_ge(t2_done, STEPS * (b + 1))
                step(V.tensor_copy(t2s[0:n, :], banks[4][0:n, :]))
                step(V.tensor_copy(t2s[64:64 + n, :], banks[4][0:n, :]))
                st.done()
                V.tensor_tensor(t2s[32:32 + n, :], banks[4][0:n, :], t2s[0:n, :].bitcast(F32), ALU.subtract)\
                    .then_inc(t2_ready, 1)

            def take_out(b, t):
                if t == 0:
                    dve.wait_ge(y_in, 16 * (b + 1))
                for n in range(2):
                    dve.wait_ge(e_done, 2 * NT * b + 2 * t + n + 1)
                    s = y[:, t, n * 512:(n + 1) * 512]
                    V.tensor_tensor(s, banks[2 * (t % 2) + n][:, :], s, ALU.add).then_inc(e_evac, 1)

            dve.wait_ge(keep_ready, 5)
            for t in range(NT):
                fold_x(0, t)
            low_rank_x(0)
            dve.wait_ge(b_ready, 2)
            V.scalar_tensor_tensor(out=b13[64:LR, :], in0=braw[64:LR, 0:I], scalar=LORA,
                                   in1=b13[64:LR, :].bitcast(F32), op0=ALU.mult, op1=ALU.subtract).then_inc(b_ready, 1)
            V.scalar_tensor_tensor(out=b2s[64:LR, :], in0=braw[64:LR, I:I + H], scalar=LORA,
                                   in1=b2s[64:LR, :].bitcast(F32), op0=ALU.mult, op1=ALU.subtract).then_inc(b_ready, 1)
            n0 = st.n
            SB = 2 * 6 + 2 + 8 + 2 * NT + 3 * NT
            with dve.Fori(0, NB - 1) as b:
                st.loop(b, SB)
                steps_2(b)
                low_rank_h(b)
                for t in range(NT):
                    fold_x(b + 1, t)
                    take_out(b, t)
                dve.wait_ge(e_evac, 2 * NT * (b + 1))
                low_rank_x(b + 1)
                norm_sums(NB + b, None)
                st.end(SB, NB - 1)
            steps_2(NB - 1)
            low_rank_h(NB - 1)
            for t in range(NT):
                take_out(NB - 1, t)
            dve.wait_ge(e_evac, 2 * NT * NB)
            norm_sums(2 * NB - 1, None)

        @block.tensor
        def _(pe):
            pe.wait_ge(consts, 2)

            def three(dst, ah, al, bh, bl, start, stop):
                nc.tensor.matmul(dst, ah, bh, start=start, stop=False)
                nc.tensor.matmul(dst, ah, bl, start=False, stop=False)
                return nc.tensor.matmul(dst, al, bh, start=False, stop=stop)

            def gate_up(b, base, xwait, done, freed):
                with pe.Fori(0, NJ // 2) as jj:
                    for q in range(2):
                        for i in range(4):
                            pe.wait_ge(lo_done, base + 8 * jj + 4 * q + i + 1)
                            for k in (2 * i, 2 * i + 1):
                                w = slice(k * CW, (k + 1) * CW)
                                for t in range(NT):
                                    if k == 0:
                                        pe.wait_ge(freed, 4 * NJ * b + 8 * jj + 4 * q + t + 1)
                                    tt = slice(t * P, (t + 1) * P)
                                    ins = three(banks[4 * q + t][:, 0:CW], xTh[:, k, tt], xTl[:, k, tt], wh[:, w],
                                                wl[:, w], k == 0, k == KH - 1)
                                    if k == KH - 1 and t < NT - 1:
                                        ins.then_inc(done, 1)
                            ins.then_inc(pe_used, 1)

            def down(b1, base):
                for c in range(NC):
                    rows = P if c < NC - 1 else LASTC
                    for n in range(2):
                        d = 2 * c + n
                        pe.wait_ge(lo_done, base + d + 1)
                        w = slice((d % 4) * 512, (d % 4 + 1) * 512)
                        for t in range(NT):
                            tt = slice(t * P, (t + 1) * P)
                            ins = three(banks[2 * t + n][:, :], hTh[0:rows, c, tt], hTl[0:rows, c, tt],
                                        wh[0:rows, w], wl[0:rows, w], c == 0, c == NC - 1)
                            if c == NC - 1 and t < NT - 1:
                                ins.then_inc(d_done, 1)
                        ins.then_inc(pe_used, 1)

            def turn(b):
                pe.wait_ge(u_freed, 8 + 4 * NJ * (b + 1))
                for c in range(NC):
                    rows = P if c < NC - 1 else LASTC
                    if c >= 8:
                        pe.wait_ge(t_lo, NC * b + c - 8 + 1)
                        pe.sem_inc(passed_pe, 1)
                    for t in range(NT):
                        ins = nc.tensor.transpose(banks[c % 8][0:rows, t * P:(t + 1) * P],
                                                  v[:, t, c * P:c * P + rows], ident[:, :])
                    ins.then_inc(t_done, 1)

            gate_up(0, NX, None, g_done, g_freed)
            pe.wait_ge(g_freed, 8 + 4 * NJ)
            gate_up(0, NX + NG, None, u_done, u_freed)
            turn(0)
            with pe.Fori(1, NB) as b:
                base = raw_base(b, False)
                pe.wait_ge(t_lo, NC * b)
                pe.sem_inc(passed_pe, 1)
                gate_up(b, base + NX, None, g_done, g_freed)
                pe.wait_ge(g_freed, 8 + 4 * NJ * (b + 1))
                pe.sem_inc(passed_pe, 1)
                down(b - 1, base + NX + NG)
                pe.wait_ge(d_evac, 8 * b)
                pe.sem_inc(passed_pe, 1)
                gate_up(b, base + NX + NG + ND, None, u_done, u_freed)
                turn(b)
            pe.wait_ge(t_lo, NC * NB)
            down(NB - 1, raw_base(NB, False))

            def turn_x(b, t):
                pe.wait_ge(xa_in[t % 2], 16 * (2 * b + t // 2 + 1))
                if not (isinstance(b, int) and b == 0 and t == 0):
                    pe.wait_ge(x1t_ready, 2 * (NT * b + t))
                for k in range(KH):
                    ins = nc.tensor.transpose(banks[5 + k // 4][:, (k % 4) * P:(k % 4 + 1) * P],
                                              xa[:, t % 2, k * P:(k + 1) * P], ident[:, :])
                ins.then_inc(x1t_done, 1)

            def low_rank(b, t):
                pe.wait_ge(x1t_ready, 2 * (NT * b + t + 1))
                if t == 0:
                    pe.sem_inc(passed_pe, 1)
                for k in range(KH):
                    ins = nc.tensor.matmul(banks[7][0:2 * R, t * P:(t + 1) * P], a13s[:, k, :], x1T[:, k, :],
                                           start=k == 0, stop=k == KH - 1)
                ins.then_inc(t1_done, 1)

            def steps_2(b):
                base = RAW2 + NW2 + NW13 * b
                pe.wait_ge(l_ready, b + 1)

                def low_h(m, frees):
                    c, q = m // Q4, m % Q4
                    rows = rows_of(c)
                    pe.wait_ge(hl_done, STEPS * b + m + 1)
                    pe.sem_inc(passed_pe, 1)
                    w = a2s[0:rows, q, c, :]
                    i1 = nc.tensor.matmul(banks[4][0:2 * R, :], w, h2h[0:rows, m % 2, :], start=m == 0, stop=False)
                    if frees:
                        i1.then_inc(pe_used, 4)
                    nc.tensor.matmul(banks[4][0:2 * R, :], w, h2l[0:rows, m % 2, :], start=False,
                                     stop=m == STEPS - 1).then_inc(t2_done, 1)

                for m in range(STEPS):
                    c, q = m // Q4, m % Q4
                    rows = rows_of(c)
                    if q == 0:
                        pe.wait_ge(lo_done, base + 4 * c + 4)
                        pe.sem_inc(passed_pe, 1)
                    for i, (low_x, done) in enumerate(((lg, gg_done), (lu, uu_done))):
                        dst = banks[2 * (m % 2) + i][0:rows, :]
                        if m >= 2:
                            pe.wait_ge((s_done, h_done)[i], STEPS * b + m - 1)
                            pe.sem_inc(passed_pe, 1)
                        for k in range(KQ):
                            s, mm = (c % 2) * 4 + 2 * i + k, slice(q * rows, (q + 1) * rows)
                            three(dst, w13h[:, s, mm], w13l[:, s, mm], xsh[:, k, :], xsl[:, k, :], k == 0, False)
                        mm = slice(q * IQ + c * P, q * IQ + c * P + rows)
                        nc.tensor.matmul(dst, b13[0:LR, mm], low_x[0:LR, :], start=False, stop=True).then_inc(done, 1)
                    if m >= 2:
                        low_h(m - 2, q == 3)
                low_h(STEPS - 2, False)
                low_h(STEPS - 1, False)

            def down_2(b, t):
                if t == 0:
                    pe.wait_ge(ql_done, CQ * (b + 1))
                    pe.sem_inc(passed_pe, 1)
                elif t >= 2:
                    pe.wait_ge(e_evac, 2 * NT * b + 2 * (t - 1))
                    pe.sem_inc(passed_pe, 1)
                tt = slice(t * P, (t + 1) * P)
                for n in range(2):
                    dst, w = banks[2 * (t % 2) + n][:, :], slice(n * 512, (n + 1) * 512)
                    for c in range(CQ):
                        rows = rows_of(c)
                        three(dst, hqh[0:rows, c, tt], hql[0:rows, c, tt], w2h[0:rows, c, w], w2l[0:rows, c, w],
                              c == 0, False)
                    if t == 0 and n == 0:
                        pe.wait_ge(t2_ready, b + 1)
                        pe.sem_inc(passed_pe, 1)
                    nc.tensor.matmul(dst, t2s[0:LR, tt], b2s[0:LR, w], start=False, stop=True).then_inc(e_done, 1)

            pe.wait_ge(small_in, 16 * 9)
            pe.wait_ge(d_evac, 8 * NB)
            for t in range(NT):
                turn_x(0, t)
                low_rank(0, t)
            pe.wait_ge(b_ready, 4)
            pe.wait_ge(a_ready, 2 * Q4)
            pe.wait_ge(keep_ready, 5)
            pe.wait_ge(lo_done, RAW2 + NW2)
            with pe.Fori(0, NB - 1) as b:
                steps_2(b)
                for t in range(NT):
                    turn_x(b + 1, t)
                    down_2(b, t)
                    low_rank(b + 1, t)
            steps_2(NB - 1)
            for t in range(NT):
                down_2(NB - 1, t)


def kernel(L0_attn_x, L0_attn_w_gate, L0_attn_w_up, L0_attn_w_down, L0_ffn_w1q, L0_ffn_a1, L0_ffn_b1, L0_ffn_w3q,
           L0_ffn_a3, L0_ffn_b3, L0_ffn_w2q, L0_ffn_a2, L0_ffn_b2):
    import numpy as np
    import concourse.bacc as bacc
    from concourse.bass_utils import run_bass_kernel_spmd as run

    x = np.asarray(L0_attn_x).reshape(TOK, H)
    xT = np.ascontiguousarray(x.reshape(NB, TB, KH, P).transpose(0, 3, 2, 1)).reshape(NB, P, KH * TB)
    xtok = np.ascontiguousarray(x.reshape(NB, NT, P, H).transpose(0, 2, 1, 3))

    def by_chunk(w):
        w = np.asarray(w).reshape(NJ, CW, KH, P)
        return np.ascontiguousarray(w.transpose(0, 3, 2, 1)).reshape(NJ, P, KH * CW)

    w = np.stack([np.asarray(L0_ffn_w1q), np.asarray(L0_ffn_w3q)]).reshape(2, Q4, IQ, KQ, P)
    full = w[:, :, :(CQ - 1) * P].reshape(2, Q4, CQ - 1, P, KQ, P)
    w13 = np.ascontiguousarray(full.transpose(2, 0, 4, 5, 1, 3)).reshape(CQ - 1, 2, KQ, P, Q4 * P)
    w13t = np.ascontiguousarray(w[:, :, (CQ - 1) * P:].transpose(0, 3, 4, 1, 2)).reshape(2, KQ, P, Q4 * LASTQ)
    a13 = np.concatenate([np.asarray(L0_ffn_a1), np.asarray(L0_ffn_a3)]).reshape(2 * R, KH, P)

    def turned(a):
        return np.ascontiguousarray(np.asarray(a).T)

    arrays = {"in_xT": xT, "in_xtok": xtok, "in_wg": by_chunk(L0_attn_w_gate), "in_wu": by_chunk(L0_attn_w_up),
              "in_wd": turned(L0_attn_w_down), "in_w13": w13, "in_w13t": w13t, "in_w2": turned(L0_ffn_w2q),
              "in_a13": np.ascontiguousarray(a13.transpose(2, 1, 0)), "in_a2": turned(L0_ffn_a2),
              "in_b1": turned(L0_ffn_b1), "in_b3": turned(L0_ffn_b3), "in_b2": turned(L0_ffn_b2)}
    nc = bacc.Bacc("TRN2", target_bir_lowering=False, num_devices=1)
    aps = [nc.dram_tensor(n, a.shape, F32, kind="ExternalInput").ap() for n, a in arrays.items()]
    o = nc.dram_tensor("out_y", (NB, P, NT, H), F32, kind="ExternalOutput").ap()
    program(nc, *aps, o)
    r = run(nc, [arrays], core_ids=[0])
    return np.ascontiguousarray(r.results[0]["out_y"].transpose(0, 2, 1, 3)).reshape(2, 1024, 1024)
```

```python
from contextlib import ExitStack

import concourse.bass as bass
from concourse import mybir

F32 = mybir.dt.float32
F32R = mybir.dt.float32r
I8 = mybir.dt.int8
I16 = mybir.dt.int16
I32 = mybir.dt.int32
ALU = mybir.AluOpType
ACT = mybir.ActivationFunctionType
AX = mybir.AxisListType
RMAX = bass.bass_isa.ReduceOp.max

P = 128
TOK, H, I = 2048, 1024, 2752
TB = 512
NB = TOK // TB
NT = TB // P
KH = H // P
CW = 344
NJ = I // CW
KEEP_FROM = I // 2
NC = -(-I // P)
LASTC = I - (NC - 1) * P
ROUNDS = 6
BIG = 1.0e30
EPS = 1e-5

NG, ND, NU = NJ * KH // 2, 2 * NC, NJ * KH // 2
USED0, USEDB = NG + NU, NG + ND + NU

Q4 = 4
HQ = H // Q4
KQ = HQ // P
IQ = I // Q4
CQ = -(-IQ // P)
LASTQ = IQ - (CQ - 1) * P
R = 2
LORA = 0.5
STEPS = CQ * Q4
LR = 96
NW2, NW13 = 2 * CQ, 4 * CQ
USED2 = USED0 + USEDB * (NB - 1) + ND


def rows_of(c):
    return P if c < CQ - 1 else LASTQ


class Steps:

    def __init__(self, eng, sem):
        self.eng, self.sem, self.base, self.n, self.outer = eng, sem, 0, 0, []

    def mark(self, ins):
        ins.then_inc(self.sem, 1)
        self.n += 1
        return self

    def done(self):
        self.eng.wait_ge(self.sem, self.base + self.n)

    def done_apart(self, passed):
        self.done()
        self.eng.sem_inc(passed, 1)

    def loop(self, i, per):
        self.outer.append((self.base, self.n))
        self.base, self.n = self.base + self.n + i * per, 0

    def end(self, per, count):
        assert self.n == per, (self.n, per)
        base, n = self.outer.pop()
        self.base, self.n = base, n + per * count


def program(nc, xT, xtok, wg, wu, wd, w13, w13t, w2, a13, a2, b1, b3, b2, out):
    x1 = nc.dram_tensor("x1", (NB, P, NT, H), F32, kind="Internal").ap()
    with ExitStack() as ctx:
        def sem(name):
            return ctx.enter_context(nc.semaphore(name))

        def bank(name):
            return ctx.enter_context(nc.psum_tensor(name, [P, 512], F32))

        room = 212600
        arena = ctx.enter_context(nc.sbuf_tensor("arena", [P, room], I8))
        start = nc.sbuf_base - room if nc.sbuf_base >= room else 0
        at = {"next": start}

        def sb(name, shape, dt, size, offset=None):
            n = size
            for d in shape[1:]:
                n *= d
            o = at["next"] if offset is None else offset
            if offset is None:
                at["next"] = -(-(o + n) // 32) * 32
                assert at["next"] <= start + room, (name, at["next"] - start)
            at[name] = o
            return nc.alloc_sbuf_tensor_at(name, shape, dt, offset=o)

        v = sb("v", [P, NT, I], F32, 4)
        hTh = sb("hTh", [P, NC, TB], F32R, 4)
        hTl = sb("hTl", [P, NC, TB], F32R, 4)
        xTh = sb("xTh", [P, KH, TB], F32R, 4)
        xTl = sb("xTl", [P, KH, TB], F32R, 4)
        wh = sb("wh", [P, 8 * CW], F32R, 4)
        wl = sb("wl", [P, 8 * CW], F32R, 4)
        x_in_place = sb("x_in_place", [P, KH, TB], F32, 4, offset=at["xTl"])
        w_in_place = sb("w_in_place", [P, 8 * CW], F32, 4, offset=at["wl"])
        sgn = sb("sgn", [P, NT, I], I8, 1)
        junkd = sb("junkd", [P, I], I8, 1)
        junka = sb("junka", [P, I // 2], I8, 1)
        ident = sb("ident", [P, P], F32, 4)
        y = sb("y", [P, NT, H], F32, 4, offset=at["hTh"])
        scr = sb("scr", [P, I // 2], F32, 4)
        mags = sb("mags", [P, NT, NJ], F32, 4)
        tc = sb("tc", [P, 2, NT], F32, 4)
        lc = sb("lc", [P, 2, NT], F32, 4)
        hc = sb("hc", [P, 2, NT], F32, 4)
        le = sb("le", [P, 2, NT], F32, 4)
        qa = sb("qa", [P, 2, NT], F32, 4)
        qb = sb("qb", [P, 2, NT], F32, 4)
        negt = sb("negt", [P, NT], F32, 4)
        ssum = sb("ssum", [P, 2, 2], F32, 4)
        sadd = sb("sadd", [P, 2], F32, 4)
        cand = sb("cand", [P, 16], F32, 4)
        top8 = sb("top8", [P, 8], F32, 4)
        pick = sb("pick", [P, 8], F32, 4)
        iota8 = sb("iota8", [P, 8], F32, 4)
        bad = sb("bad", [P, 1], F32, 4)
        flag = sb("flag", [P, 1], F32, 4)
        bit = sb("bit", [P, NT], I32, 4)
        taken = sb("taken", [P, NT], I32, 4)
        carry = sb("carry", [P, 1], F32, 4)
        stats = sb("stats", [P, NT, 2, 6], F32, 4)
        mv = sb("mv", [P, NT, 2], F32, 4)
        ve = sb("ve", [P, NT], F32, 4)
        mhalf = sb("mhalf", [P, NT], F32, 4)
        rstd = sb("rstd", [P, NT], F32, 4)
        nbias = sb("nbias", [P, NT], F32, 4)

        over = {"at": at["v"]}

        def put(name, shape, dt):
            n = 4
            for d in shape[1:]:
                n *= d
            o = over["at"]
            over["at"] = -(-(o + n) // 32) * 32
            return sb(name, shape, dt, 4, offset=o)

        w2h = put("w2h", [P, CQ, H], F32R)
        b13 = put("b13", [P, I], F32R)
        b2s = put("b2s", [P, H], F32R)
        a2s = put("a2s", [P, Q4, CQ, 2 * R], F32R)
        a2raw = put("a2raw", [P, Q4, CQ, R], F32)
        a13s = put("a13s", [P, KH, 2 * R], F32)
        keep = put("keep", [P, 2], F32)
        t2s = put("t2s", [P, TB], F32R)
        assert over["at"] <= at["hTh"]
        over["at"] = at["xTh"]
        w2l = put("w2l", [P, CQ, H], F32R)
        w2_in_place = sb("w2_in_place", [P, CQ, H], F32, 4, offset=at["w2l"])
        xa = put("xa", [P, 2, H], F32)
        assert over["at"] <= at["wh"]
        over["at"] = at["hTh"] + NT * H * 4
        w13h = put("w13h", [P, 8, 512], F32R)
        w13l = put("w13l", [P, 8, 512], F32R)
        w13_in_place = sb("w13_in_place", [P, 8, 512], F32, 4, offset=at["w13l"])
        x1T = put("x1T", [P, KH, P], F32)
        xf = put("xf", [P, KQ, P], F32)
        xsh = put("xsh", [P, KQ, TB], F32R)
        xsl = put("xsl", [P, KQ, TB], F32R)
        lg = put("lg", [P, TB], F32R)
        lu = put("lu", [P, TB], F32R)
        th = put("th", [P, TB], F32R)
        tl = put("tl", [P, TB], F32R)
        over_bt = over["at"]
        sg = put("sg", [P, 2, TB], F32)
        h2 = put("h2", [P, 2, TB], F32)
        h2h = put("h2h", [P, 2, TB], F32R)
        h2l = put("h2l", [P, 2, TB], F32R)
        fold = put("fold", [P, TB], F32)
        assert over["at"] <= at["xTh"]
        over["at"] = over_bt
        braw = put("braw", [P, I + H], F32)
        over["at"] = at["wh"]
        hqh = put("hqh", [P, CQ, TB], F32R)
        hql = put("hql", [P, CQ, TB], F32R)
        assert over["at"] <= at["junkd"]

        banks = [bank(f"bank{i}") for i in range(8)]

        raw_in = [sem(f"raw_in{i}") for i in range(4)]
        x_raw = [sem(f"x_raw{i}") for i in range(KH)]
        x_hi, x_lo = sem("x_hi"), sem("x_lo")
        w2_raw = [sem(f"w2_raw{i}") for i in range(NW2)]
        w2_hi, w2_lo = sem("w2_hi"), sem("w2_lo")
        hi_done, lo_done, pe_used = sem("hi_done"), sem("lo_done"), sem("pe_used")
        g_done, g_freed = sem("g_done"), sem("g_freed")
        u_done, u_freed = sem("u_done"), sem("u_freed")
        t_done, t_hi, t_lo = sem("t_done"), sem("t_hi"), sem("t_lo")
        d_done, d_evac = sem("d_done"), sem("d_evac")
        probe, signs = sem("probe"), sem("signs")
        bad_ready, flag_ready = sem("bad_ready"), sem("flag_ready")
        x_in, ve_ready, rstd_ready, nb_ready, norm_done, x1_out = (
            sem("x_in"), sem("ve_ready"), sem("rstd_ready"), sem("nb_ready"), sem("norm_done"), sem("x1_out"))
        xa_in = [sem(f"xa_in{i}") for i in range(2)]
        small_in, b_zero, b_in, b_ready, a_ready, keep_ready = (
            sem("small_in"), sem("b_zero"), sem("b_in"), sem("b_ready"), sem("a_ready"), sem("keep_ready"))
        l_fold = sem("l_fold")
        x1t_done, x1t_ready, t1_done, l_ready = sem("x1t_done"), sem("x1t_ready"), sem("t1_done"), sem("l_ready")
        gg_done, uu_done, s_done, h_done, f_done = (
            sem("gg_done"), sem("uu_done"), sem("s_done"), sem("h_done"), sem("f_done"))
        hh_done, hl_done, t2_done, t2_ready = sem("hh_done"), sem("hl_done"), sem("t2_done"), sem("t2_ready")
        qh_done, ql_done, e_done, e_evac, y_in, out_done = (
            sem("qh_done"), sem("ql_done"), sem("e_done"), sem("e_evac"), sem("y_in"), sem("out_done"))
        passed_dve, passed_pool, passed_pe, passed_sp = (
            sem("passed_dve"), sem("passed_pool"), sem("passed_pe"), sem("passed_sp"))
        exact_s = sem("exact_s")
        consts, dve_s, act_s, pool_s = sem("consts"), sem("dve_s"), sem("act_s"), sem("pool_s")

        block = ctx.enter_context(nc.Block())

        def used_base(b, first):
            return 0 if first else USED0 + USEDB * (b - 1)

        def landed(base, i):
            return 4 * base + 16 * (i // 4) + 16

        def free_g(i, b, first):
            return (used_base(b, first) + i - 4 + 1) if (i >= 4 or not first) else None

        def free_d(i, base):
            return base + i - 4 + 1

        def free_u(i, base, first):
            if first or i >= 4:
                return base + i - 4 + 1
            return base - 4 + min(i + 1, 3) + 1

        @block.sync
        def _(sp):
            def load(slot, dst, src, free):
                if free is not None:
                    sp.wait_ge(pe_used, free)
                sp.sem_inc(passed_sp, 1)
                sp.dma_start(dst, src).then_inc(raw_in[slot], 16)

            def load_gu_piece(w, chunk, i, free):
                c, s = i % 4 * 2 * CW, slice(i % 4 * 2 * CW, (i % 4 + 1) * 2 * CW)
                load(i % 4, w_in_place[:, s],
                     w[bass.ds(chunk, 1), :, c:c + 2 * CW].rearrange("o p n -> (o p) n"), free)

            def load_head(b, base, first):
                for i in range(4):
                    for k in (2 * i, 2 * i + 1):
                        if not first:
                            sp.wait_ge(pe_used, base - 4 + i + 1)
                        sp.sem_inc(passed_sp, 1)
                        sp.dma_start(x_in_place[:, k, :], xT[bass.ds(b, 1), :, k * TB:(k + 1) * TB]
                                     .rearrange("o p n -> (o p) n")).then_inc(x_raw[k], 16)
                    load_gu_piece(wg, 0, i, None if first else base - 4 + i + 1)

            def load_gu(w, base):
                with sp.Fori(0, NJ // 2 - 1) as jj:
                    for i in range(4, 12):
                        load_gu_piece(w, 2 * jj + i // 4, i, base + 8 * jj + i - 3)
                for i in range(NG - 4, NG):
                    load_gu_piece(w, NJ - 1, i, base + i - 3)

            def load_u(base, first):
                for i in range(4):
                    load_gu_piece(wu, 0, i, free_u(i, base, first))
                load_gu(wu, base)

            def load_d(base, between=None):
                def piece(c, d, free, rows=P):
                    s = slice(d % 4 * 512, (d % 4 + 1) * 512)
                    load(d % 4, w_in_place[0:rows, s], wd[bass.ds(c * P, rows), d % 2 * 512:(d % 2 + 1) * 512], free)
                for d in range(4):
                    piece(d // 2, d, free_d(d, base))
                if between is not None:
                    between()
                with sp.Fori(1, ND // 4 - 1) as g:
                    for d in range(4):
                        piece(2 * g + d // 2, d, base + 4 * g + d - 3)
                for d in range(ND - 4, ND):
                    piece(d // 2, d, base + d - 3, P if d < ND - 2 else LASTC)

            def x_tiles(b1, used):
                sp.wait_ge(pe_used, used)
                sp.sem_inc(passed_sp, 1)
                sp.dma_start(y[:, :, :], xtok[bass.ds(b1, 1), :, :, :].rearrange("o p t h -> (o p) t h"))\
                    .then_inc(x_in, 16)

            load_head(0, 0, True)
            load_gu(wg, 0)
            load_u(NG, True)
            with sp.Fori(1, NB) as b:
                base = used_base(b, False)
                load_head(b, base, False)
                load_gu(wg, base)
                load_d(base + NG)
                x_tiles(b - 1, base + NG + 16)
                load_u(base + NG + ND, False)

            def load_w2():
                for d in range(NW2):
                    rows = rows_of(d // 2)
                    sp.dma_start(w2_in_place[0:rows, d // 2, (d % 2) * 512:(d % 2 + 1) * 512],
                                 w2[d // 2 * P:d // 2 * P + rows, (d % 2) * 512:(d % 2 + 1) * 512]).then_inc(w2_raw[d], 16)

            load_d(used_base(NB, False), load_w2)
            x_tiles(NB - 1, used_base(NB, False) + 16)
            sp.wait_ge(t_done, NC * NB)
            sp.dma_start(a13s[:, :, :], a13).then_inc(small_in, 16)
            for q in range(Q4):
                for c0, n in ((0, CQ - 1), (CQ - 1, 1)):
                    rows = rows_of(c0)
                    sp.dma_start(a2raw[0:rows, q, c0:c0 + n, :],
                                 a2[q * IQ + c0 * P:q * IQ + c0 * P + n * rows, :].rearrange("(c p) r -> p c r", p=rows))\
                        .then_inc(small_in, 16)
            sp.wait_ge(b_zero, 1)
            for g in range(3):
                for i, (src, c0) in enumerate(((b1, 0), (b3, 0), (b2, I), (b2, I))):
                    r0 = 32 * g + R * (i % 2)
                    sp.dma_start(braw[r0:r0 + R, c0:c0 + src.shape[1]], src).then_inc(b_in, 16)

            def load_xa(b):
                sp.wait_ge(x1_out, 16 * NT * (b + 1))
                for t in range(NT):
                    if t >= 2 or not (isinstance(b, int) and b == 0):
                        sp.wait_ge(x1t_done, NT * b + t - 1)
                    sp.sem_inc(passed_sp, 1)
                    sp.dma_start(xa[:, t % 2, :], x1[bass.ds(b, 1), :, t, :].rearrange("o p h -> (o p) h"))\
                        .then_inc(xa_in[t % 2], 16)

            def load_13(b, chunks):
                base = USED2 + NW13 * b
                for c in chunks:
                    first = isinstance(b, int) and b == 0
                    for i in range(4):
                        w, k = i // 2, i % 2
                        s, m = (c % 2) * 4 + i, Q4 * rows_of(c)
                        if first and c < 2:
                            sp.wait_ge(pe_used, USED2)
                        else:
                            sp.wait_ge(pe_used, base + 4 * (c - 1))
                        if not (first and c == 0):
                            sp.sem_inc(passed_sp, 1)
                            sp.wait_ge(hi_done, base + 4 * (c - 1) + i + 1)
                        sp.sem_inc(passed_sp, 1)
                        sp.dma_start(w13_in_place[:, s, 0:m], w13[c, w, k] if c < CQ - 1 else w13t[w, k])\
                            .then_inc(raw_in[i], 16)

            def load_y(b):
                sp.wait_ge(x1_out, 16 * NT * NB)
                if isinstance(b, int) and b == 0:
                    pass
                else:
                    sp.wait_ge(out_done, 16 * NT * b)
                sp.sem_inc(passed_sp, 1)
                sp.dma_start(y[:, :, :], x1[bass.ds(b, 1), :, :, :].rearrange("o p t h -> (o p) t h"))\
                    .then_inc(y_in, 16)

            load_13(0, (0,))
            load_xa(0)
            load_13(0, range(1, CQ))
            load_y(0)
            with sp.Fori(1, NB) as b:
                load_13(b, (0,))
                load_xa(b)
                load_13(b, range(1, CQ))
                load_y(b)
            sp.wait_ge(out_done, 16 * NT * NB)

        @block.gpsimd
        def _(pool):
            nc.gpsimd.memset(ident[:], 0.0).then_inc(pool_s, 1)
            pool.wait_ge(pool_s, 1)
            nc.gpsimd.affine_select(out=ident[:], in_=ident[:], compare_op=ALU.not_equal, fill=1.0, base=0,
                                    pattern=[[-1, P]], channel_multiplier=1).then_inc(consts, 1)
            nc.gpsimd.iota(iota8[:], pattern=[[1, 8]], base=0, channel_multiplier=0,
                           allow_small_or_imprecise_dtypes=True).then_inc(consts, 1)
            nc.gpsimd.memset(mhalf[:], -0.5).then_inc(pool_s, 1)
            pool.wait_ge(pool_s, 2)

            def less(hi, lo, landed, done):
                nc.gpsimd.tensor_tensor(lo, landed, hi.bitcast(F32), ALU.subtract).then_inc(done, 1)

            def low(n, hi, lo, landed):
                pool.wait_ge(hi_done, n + 1)
                less(hi, lo, landed, lo_done)

            def low_gu_piece(n, i):
                s = slice((i % 4) * 2 * CW, (i % 4 + 1) * 2 * CW)
                low(n, wh[:, s], wl[:, s], w_in_place[:, s])

            def low_head(b, base):
                for i in range(4):
                    for k in (2 * i, 2 * i + 1):
                        pool.wait_ge(x_hi, KH * b + k + 1)
                        less(xTh[:, k, :], xTl[:, k, :], x_in_place[:, k, :], x_lo)
                    low_gu_piece(base + i, i)

            def low_gu(base, given=0):
                for i in range(given, 8):
                    low_gu_piece(base + i, i)
                with pool.Fori(1, NJ // 2) as jj:
                    for i in range(8):
                        low_gu_piece(base + 8 * jj + i, i)

            def low_d(base):
                def one(n, d, rows):
                    s = slice((d % 4) * 512, (d % 4 + 1) * 512)
                    low(n, wh[0:rows, s], wl[0:rows, s], w_in_place[0:rows, s])
                with pool.Fori(0, NC // 2 - 1) as c:
                    for d in range(4):
                        one(base + 4 * c + d, d, P)
                for d in range(4):
                    one(base + ND - 4 + d, d, P if d < 2 else LASTC)

            def flagged(b):
                pool.wait_ge(bad_ready, b + 1)
                pool.sem_inc(passed_pool, 1)
                nc.gpsimd.partition_all_reduce(flag[:, 0:1], bad[:, 0:1], P, RMAX).then_inc(flag_ready, 1)

            def inv_std(b1):
                pool.wait_ge(ve_ready, b1 + 1)
                nc.gpsimd.tensor_tensor(rstd[:], ve[:], mhalf[:], ALU.pow).then_inc(rstd_ready, 1)

            low_head(0, 0)
            low_gu(0, 4)
            for i in range(8):
                low_gu_piece(NG + i, i)
            flagged(0)
            with pool.Fori(1, NJ // 2) as jj:
                for i in range(8):
                    low_gu_piece(NG + 8 * jj + i, i)
            with pool.Fori(1, NB) as b:
                base = used_base(b, False)
                low_head(b, base)
                low_gu(base, 4)
                low_d(base + NG)
                flagged(b)
                inv_std(b - 1)
                low_gu(base + NG + ND)
            low_d(used_base(NB, False))
            for d in range(NW2):
                c, s, rows = d // 2, slice((d % 2) * 512, (d % 2 + 1) * 512), rows_of(d // 2)
                pool.wait_ge(w2_hi, d + 1)
                less(w2h[0:rows, c, s], w2l[0:rows, c, s], w2_in_place[0:rows, c, s], w2_lo)
            inv_std(NB - 1)
            nc.gpsimd.memset(keep[:], 1.0).then_inc(pool_s, 1)
            pool.wait_ge(pool_s, 3)
            nc.gpsimd.affine_select(out=keep[:, 0:1], in_=keep[:, 0:1], compare_op=ALU.is_ge, fill=0.0, base=R - 1,
                                    pattern=[[0, 1]], channel_multiplier=-1).then_inc(keep_ready, 1)
            nc.gpsimd.affine_select(out=keep[:, 1:2], in_=keep[:, 1:2], compare_op=ALU.is_ge, fill=0.0, base=-R,
                                    pattern=[[0, 1]], channel_multiplier=1).then_inc(keep_ready, 1)
            pool.wait_ge(pe_used, USED2)
            nc.gpsimd.memset(braw[0:LR, :], 0.0).then_inc(b_zero, 1)
            for i, z in enumerate((lg, lu, t2s)):
                nc.gpsimd.memset(z[0:LR, :].bitcast(F32), 0.0).then_inc(keep_ready, 1)

            def low_13(b, c, i):
                s, m = (c % 2) * 4 + i, Q4 * rows_of(c)
                low(USED2 + NW13 * b + 4 * c + i, w13h[:, s, 0:m], w13l[:, s, 0:m], w13_in_place[:, s, 0:m])

            def steps_2(b, last):
                def low_h(m):
                    rows = rows_of(m // Q4)
                    pool.wait_ge(hh_done, STEPS * b + m + 1)
                    nc.gpsimd.tensor_tensor(h2l[0:rows, m % 2, :], h2[0:rows, m % 2, :],
                                            h2h[0:rows, m % 2, :].bitcast(F32), ALU.subtract).then_inc(hl_done, 1)

                def low_q(c):
                    rows = rows_of(c)
                    pool.wait_ge(qh_done, CQ * b + c + 1)
                    nc.gpsimd.tensor_tensor(hql[0:rows, c, :], fold[0:rows, :], hqh[0:rows, c, :].bitcast(F32),
                                            ALU.subtract).then_inc(ql_done, 1)

                for m in range(STEPS):
                    c, q = m // Q4, m % Q4
                    if c < CQ - 1:
                        low_13(b, c + 1, q)
                    elif not last:
                        low_13(b + 1, 0, q)
                    if m:
                        low_h(m - 1)
                    if q == 0 and c:
                        low_q(c - 1)
                low_h(STEPS - 1)
                low_q(CQ - 1)

            for i in range(4):
                low_13(0, 0, i)
            with pool.Fori(0, NB - 1) as b:
                steps_2(b, False)
                inv_std(NB + b)
            steps_2(NB - 1, True)
            inv_std(2 * NB - 1)

        @block.scalar
        def _(act):
            st = Steps(act, act_s)

            def high(count, slot, hi, piece):
                act.wait_ge(raw_in[slot], count)
                nc.scalar.copy(hi, piece).then_inc(hi_done, 1)

            def high_gu_piece(count, i):
                s = slice((i % 4) * 2 * CW, (i % 4 + 1) * 2 * CW)
                high(count, i % 4, wh[:, s], w_in_place[:, s])

            def high_d(base, d):
                rows = P if d < ND - 2 else LASTC
                s = slice((d % 4) * 512, (d % 4 + 1) * 512)
                high(landed(base, d), d % 4, wh[0:rows, s], w_in_place[0:rows, s])

            def head(b, base):
                for i in range(4):
                    for k in (2 * i, 2 * i + 1):
                        act.wait_ge(x_raw[k], 16 * b + 16)
                        nc.scalar.copy(xTh[:, k, :], x_in_place[:, k, :]).then_inc(x_hi, 1)
                    high_gu_piece(landed(base, i), i)

            def evac(b, j, p, base):
                for t in range(NT):
                    if t < NT - 1:
                        act.wait_ge(g_done, 3 * NJ * b + 3 * j + t + 1)
                    else:
                        act.wait_ge(pe_used, base + 4 * j + 4)
                    nc.scalar.activation(v[:, t, bass.ds(j * CW, CW)], banks[4 * p + t][:, 0:CW], ACT.Silu)\
                        .then_inc(g_freed, 1)

            def gate(b, base, first):
                if not first:
                    act.wait_ge(t_done, NC * b)

                def ahead(jj, q):
                    for i in range(4 * q + 4, 4 * q + 8):
                        high_gu_piece(landed(base + 8 * jj, i), i)

                with act.Fori(0, NJ // 2 - 1) as jj:
                    for q in range(2):
                        ahead(jj, q)
                        evac(b, 2 * jj + q, q, base)
                ahead(NJ // 2 - 1, 0)
                evac(b, NJ - 2, 0, base)

            def search(b, piece):
                for r in range(ROUNDS):
                    act.wait_ge(probe, ROUNDS * b + r + 1)
                    for t in (2, 3):
                        for h in range(2):
                            st.done()
                            ins = nc.scalar.activation(junka[:, :], v[:, t, h * (I // 2):(h + 1) * (I // 2)], ACT.Sign,
                                                       bias=negt[:, t:t + 1], accum_out=ssum[:, t - 2, h:h + 1])
                            st.mark(ins)
                            if t == 2 or h == 0:
                                piece()
                    st.done()
                    act.sem_inc(signs, 1)
                    piece()

            def up(base, given):
                for i in range(given, 8):
                    high_gu_piece(landed(base, i), i)
                with act.Fori(1, NJ // 2) as jj:
                    for i in range(8):
                        high_gu_piece(landed(base + 8 * jj, i), i)

            def turned(b):
                for c in range(NC):
                    rows = P if c < NC - 1 else LASTC
                    act.wait_ge(t_done, NC * b + c + 1)
                    if c == 0:
                        act.wait_ge(x1_out, 16 * NT * b)
                    nc.scalar.copy(hTh[0:rows, c, :], banks[c % 8][0:rows, :]).then_inc(t_hi, 1)

            def norm(b1, n, dst, sent):
                act.wait_ge(nb_ready, n + 1)
                for t in range(NT):
                    nc.scalar.activation(y[:, t, :], y[:, t, :], ACT.Identity, scale=rstd[:, t:t + 1],
                                         bias=nbias[:, t:t + 1]).then_inc(norm_done, 1)
                for t in range(NT):
                    act.wait_ge(norm_done, NT * n + t + 1)
                    act.dma_start(dst[bass.ds(b1, 1), :, t, :].rearrange("o p h -> (o p) h"), y[:, t, :])\
                        .then_inc(sent, 16)

            head(0, 0)
            gate(0, 0, True)
            for i in range(4):
                high_gu_piece(landed(NG, i), i)
            evac(0, NJ - 1, 1, 0)
            ahead_u = list(range(4, 8))
            search(0, lambda: ahead_u and high_gu_piece(landed(NG, ahead_u[0]), ahead_u.pop(0)))
            up(NG, 8)

            def block_1(b, last):
                base = used_base(b, False)
                gate(b, base, False)
                for d in range(4):
                    high_d(base + NG, d)
                evac(b, NJ - 1, 1, base)
                ahead_d = list(range(4, ND))
                search(b, lambda: high_d(base + NG, ahead_d.pop(0)))
                for d in ahead_d:
                    high_d(base + NG, d)
                up(base + NG + ND, 0)
                norm(b - 1, b - 1, x1, x1_out)
                if not last:
                    head(b + 1, base + USEDB)
                turned(b)

            head(1, USED0)
            turned(0)
            with act.Fori(1, NB - 1) as b:
                st.loop(b - 1, 4 * ROUNDS)
                block_1(b, False)
                st.end(4 * ROUNDS, NB - 2)
            block_1(NB - 1, True)
            for d in range(ND):
                high_d(used_base(NB, False), d)
            act.wait_ge(t_done, NC * NB)
            for d in range(NW2):
                c, s, rows = d // 2, slice((d % 2) * 512, (d % 2 + 1) * 512), rows_of(d // 2)
                act.wait_ge(w2_raw[d], 16)
                nc.scalar.copy(w2h[0:rows, c, s], w2_in_place[0:rows, c, s]).then_inc(w2_hi, 1)
            norm(NB - 1, NB - 1, x1, x1_out)

            def high_13(b, c, i):
                s, m = (c % 2) * 4 + i, Q4 * rows_of(c)
                high(4 * (USED2 + NW13 * b) + 16 * (c + 1), i, w13h[:, s, 0:m], w13_in_place[:, s, 0:m])

            def turned_x(b, t):
                act.wait_ge(x1t_done, NT * b + t + 1)
                if not (isinstance(b, int) and b == 0 and t == 0):
                    act.wait_ge(t1_done, NT * b + t)
                    act.wait_ge(l_fold, NT * b + t)
                for i in range(2):
                    nc.scalar.copy(x1T[:, 4 * i:4 * i + 4, :].rearrange("p k t -> p (k t)"), banks[5 + i][:, :])\
                        .then_inc(x1t_ready, 1)

            def steps_2(b, last):
                def high_h(m):
                    rows = rows_of(m // Q4)
                    act.wait_ge(h_done, STEPS * b + m + 1)
                    if m >= 2:
                        act.wait_ge(t2_done, STEPS * b + m - 1)
                    nc.scalar.copy(h2h[0:rows, m % 2, :], h2[0:rows, m % 2, :]).then_inc(hh_done, 1)

                def high_q(c):
                    rows = rows_of(c)
                    act.wait_ge(f_done, CQ * b + c + 1)
                    nc.scalar.copy(hqh[0:rows, c, :], fold[0:rows, :]).then_inc(qh_done, 1)

                for m in range(STEPS):
                    c, q = m // Q4, m % Q4
                    if c < CQ - 1:
                        high_13(b, c + 1, q)
                    elif not last:
                        high_13(b + 1, 0, q)
                    rows = rows_of(c)
                    act.wait_ge(gg_done, STEPS * b + m + 1)
                    if m >= 2:
                        act.wait_ge(h_done, STEPS * b + m - 1)
                    nc.scalar.activation(sg[0:rows, m % 2, :], banks[2 * (m % 2)][0:rows, :], ACT.Silu).then_inc(s_done, 1)
                    if m:
                        high_h(m - 1)
                    if q == 0 and c:
                        high_q(c - 1)
                high_h(STEPS - 1)
                high_q(CQ - 1)

            for i in range(4):
                high_13(0, 0, i)
            for t in range(NT):
                turned_x(0, t)
            act.wait_ge(b_in, 16 * 12)
            nc.scalar.mul(b13[0:LR, :], braw[0:LR, 0:I], LORA).then_inc(b_ready, 1)
            nc.scalar.mul(b2s[0:LR, :], braw[0:LR, I:I + H], LORA).then_inc(b_ready, 1)
            with act.Fori(0, NB - 1) as b:
                steps_2(b, False)
                for t in range(NT):
                    turned_x(b + 1, t)
                norm(b, NB + b, out, out_done)
            steps_2(NB - 1, True)
            norm(NB - 1, 2 * NB - 1, out, out_done)

        @block.vector
        def _(dve):
            st = Steps(dve, dve_s)
            es = Steps(dve, exact_s)
            EXACT = 2 + 31 * (5 + NT) + NT + 1 + NT * (1 + 7 * NJ)
            V = nc.vector
            dve.sem_inc(g_freed, 8)
            dve.sem_inc(u_freed, 8)
            dve.wait_ge(consts, 2)

            def step(ins):
                st.mark(ins)

            def take_gate(b):
                with dve.Fori(0, NJ // 2) as jj:
                    st.loop(jj, 16)
                    for q in range(2):
                        for t in range(NT):
                            dve.wait_ge(g_freed, 8 + 4 * NJ * b + 8 * jj + 4 * q + t + 1)
                            s = v[:, t, bass.ds((2 * jj + q) * CW, CW)]
                            step(V.tensor_scalar(sgn[:, t, bass.ds((2 * jj + q) * CW, CW)], s, 0.0, 2.0,
                                                 ALU.is_ge, ALU.mult))
                            st.done()
                            step(V.scalar_tensor_tensor(out=s, in0=s, scalar=-1.0, in1=s, op0=ALU.mult, op1=ALU.max,
                                                        accum_out=mags[:, t, bass.ds(2 * jj + q, 1)]))
                    st.end(16, NJ // 2)

            def say_probe():
                st.done()
                V.tensor_scalar(negt[:], tc[:, 0, :], -1.0, None, ALU.mult).then_inc(probe, 1)

            def count(b, r):
                say_probe()
                for t in (0, 1):
                    step(V.tensor_scalar(junkd[:, :], v[:, t, :], tc[:, 0, t:t + 1], None, ALU.is_lt, ALU.add,
                                         accum_out=tc[:, 1, t:t + 1]))
                    st.done()
                dve.wait_ge(signs, ROUNDS * b + r + 1)
                step(V.tensor_tensor(sadd[:], ssum[:, :, 0], ssum[:, :, 1], ALU.add))
                st.done()
                step(V.tensor_scalar(sadd[:], sadd[:], -0.5, I / 2 - 0.25, ALU.mult, ALU.add))
                st.done()
                step(V.tensor_scalar(tc[:, 1, 2:4], sadd[:], 12582912.0, -12582912.0, ALU.add, ALU.add))
                st.done()

            def search(b):
                st.done()
                step(V.tensor_reduce(le[:, 0, :], mags[:], AX.X, ALU.add))
                st.done()
                step(V.tensor_scalar(tc[:, 0, :], le[:, 0, :], 0.75 / I, None, ALU.mult))
                step(V.memset(lc[:], 0.0))
                step(V.tensor_scalar(hc[:, 0, :], le[:, 0, :], 2.001 / I, None, ALU.mult))
                step(V.memset(hc[:, 1, :], float(I)))
                for r in range(ROUNDS):
                    count(b, r)
                    step(V.tensor_scalar(le[:], tc[:, 1:2, :].broadcast_to((P, 2, NT)), KEEP_FROM + 0.5, None, ALU.is_le))
                    st.done()
                    step(V.scalar_tensor_tensor(out=qa[:], in0=le[:], scalar=BIG, in1=tc[:], op0=ALU.mult, op1=ALU.max))
                    step(V.scalar_tensor_tensor(out=qb[:], in0=le[:], scalar=BIG, in1=tc[:], op0=ALU.mult, op1=ALU.min))
                    st.done()
                    step(V.tensor_tensor(hc[:], hc[:], qa[:], ALU.min))
                    step(V.tensor_tensor(lc[:], lc[:], qb[:], ALU.max))
                    st.done()
                    if r == ROUNDS - 1:
                        break
                    step(V.tensor_tensor(qa[:], hc[:], lc[:], ALU.subtract))
                    step(V.tensor_scalar(qb[:, 0, :], lc[:, 1, :], -1.0, KEEP_FROM + 4.0, ALU.mult, ALU.add))
                    st.done()
                    step(V.reciprocal(qb[:, 1, :], qa[:, 1, :]))
                    step(V.tensor_tensor(qa[:, 0, :], qa[:, 0, :], qb[:, 0, :], ALU.mult))
                    st.done()
                    step(V.tensor_tensor(qa[:, 0, :], qa[:, 0, :], qb[:, 1, :], ALU.mult))
                    st.done()
                    step(V.tensor_tensor(tc[:, 0, :], qa[:, 0, :], lc[:, 0, :], ALU.add))
                step(V.tensor_scalar(qa[:, 0, :], hc[:, 1, :], -(KEEP_FROM + 1.0), None, ALU.add))
                Q = I // 2
                for t in range(NT):
                    for c in range(2):
                        st.done()
                        step(V.scalar_tensor_tensor(out=scr[:], in0=v[:, t, c * Q:(c + 1) * Q], scalar=hc[:, 0, t:t + 1],
                                                    in1=v[:, t, c * Q:(c + 1) * Q], op0=ALU.is_lt, op1=ALU.mult))
                        st.done_apart(passed_dve)
                        step(V.max(out=cand[:, 8 * c:8 * c + 8], in_=scr[:]))
                    st.done_apart(passed_dve)
                    step(V.max(out=top8[:], in_=cand[:]))
                    st.done()
                    step(V.scalar_tensor_tensor(out=pick[:], in0=iota8[:], scalar=qa[:, 0, t:t + 1], in1=top8[:],
                                                op0=ALU.is_equal, op1=ALU.mult, accum_out=tc[:, 0, t:t + 1]))
                    st.done()
                    step(V.tensor_scalar(junkd[:, :], v[:, t, :], tc[:, 0, t:t + 1], None, ALU.is_lt, ALU.add,
                                         accum_out=tc[:, 1, t:t + 1]))
                st.done()
                step(V.tensor_scalar(le[:, 0, :], tc[:, 1, :], float(KEEP_FROM), None, ALU.not_equal))
                st.done()
                V.tensor_reduce(bad[:], le[:, 0, :], AX.X, ALU.max).then_inc(bad_ready, 1)
                dve.wait_ge(flag_ready, b + 1)
                dve.sem_inc(passed_dve, 1)
                flagged = dve.value_load(flag[0:1, 0:1].bitcast(I32))
                with dve.If(flagged != 0):
                    exact()
                with dve.Else():
                    dve.sem_inc(exact_s, EXACT)

            def exact():
                found, trial = tc[:, 0, :].bitcast(I32), le[:, 0, :].bitcast(I32)
                es.mark(V.memset(found, 0))
                es.mark(V.memset(bit[:], 1 << 30))
                with dve.Fori(0, 31) as i:
                    es.loop(i, 5 + NT)
                    es.done()
                    es.mark(V.tensor_tensor(trial, found, bit[:], ALU.bitwise_or))
                    es.done()
                    for t in range(NT):
                        es.mark(V.tensor_scalar(junkd[:, :], v[:, t, :], le[:, 0, t:t + 1], None, ALU.is_lt, ALU.add,
                                                accum_out=tc[:, 1, t:t + 1]))
                        es.done()
                    es.mark(V.tensor_scalar(taken[:], tc[:, 1, :], KEEP_FROM - 0.5, None, ALU.is_lt))
                    es.done()
                    es.mark(V.tensor_tensor(taken[:], taken[:], bit[:], ALU.mult))
                    es.done()
                    es.mark(V.tensor_tensor(found, found, taken[:], ALU.bitwise_or))
                    es.mark(V.tensor_scalar(bit[:], bit[:], 1, None, ALU.logical_shift_right))
                    es.end(5 + NT, 31)
                es.done()
                for t in range(NT):
                    es.mark(V.tensor_scalar(junkd[:, :], v[:, t, :], tc[:, 0, t:t + 1], None, ALU.is_lt, ALU.add,
                                            accum_out=tc[:, 1, t:t + 1]))
                    es.done()
                es.mark(V.tensor_scalar(qa[:, 0, :], tc[:, 1, :], -1.0, float(KEEP_FROM), ALU.mult, ALU.add))
                eq, nth = scr[:, 0:CW], scr[:, CW:2 * CW]
                for t in range(NT):
                    es.mark(V.memset(carry[:], 0.0))
                    with dve.Fori(0, NJ) as j:
                        es.loop(j, 7)
                        es.done()
                        g = sgn[:, t, bass.ds(j * CW, CW)]
                        es.mark(V.tensor_scalar(eq, v[:, t, bass.ds(j * CW, CW)], tc[:, 0, t:t + 1], None, ALU.is_equal))
                        es.done()
                        es.mark(V.tensor_tensor_scan(nth, eq, eq, carry[:, 0:1], ALU.add, ALU.max))
                        es.done()
                        es.mark(V.tensor_copy(carry[:], nth[:, CW - 1:CW]))
                        es.mark(V.scalar_tensor_tensor(out=eq, in0=nth, scalar=qa[:, 0, t:t + 1], in1=eq, op0=ALU.is_le,
                                                       op1=ALU.mult))
                        es.done()
                        es.mark(V.tensor_scalar(eq, eq, -1.0, 1.0, ALU.mult, ALU.add))
                        es.done()
                        es.mark(V.scalar_tensor_tensor(out=g, in0=g, scalar=-1.0, in1=eq, op0=ALU.add, op1=ALU.mult))
                        es.done()
                        es.mark(V.tensor_scalar(g, g, 1.0, None, ALU.add))
                        es.end(7, NJ)
                es.done_apart(passed_dve)
                assert es.n == EXACT

            def take_down(b1, used):
                dve.wait_ge(x_in, 16 * (b1 + 1))
                for n in range(2):
                    for t in range(NT):
                        if t < NT - 1:
                            dve.wait_ge(d_done, 6 * b1 + 3 * n + t + 1)
                        else:
                            dve.wait_ge(pe_used, used + ND - 1 + n)
                        s = y[:, t, n * 512:(n + 1) * 512]
                        V.tensor_tensor(s, banks[2 * t + n][:, :], s, ALU.add).then_inc(d_evac, 1)
                dve.wait_ge(d_evac, 8 * (b1 + 1))
                norm_sums(b1, None)

            def norm_sums(n, ready):
                for t in range(NT):
                    for i in range(2):
                        step(V.bn_stats(stats[:, t, i, :], y[:, t, i * 512:(i + 1) * 512]))
                    st.done_apart(passed_dve)
                    step(V.bn_aggr(mv[:, t, :], stats[:, t, :, :].rearrange("p n s -> p (n s)")))
                st.done()
                V.tensor_scalar(ve[:], mv[:, :, 1], EPS, None, ALU.add).then_inc(ve_ready, 1)
                dve.wait_ge(rstd_ready, n + 1)
                V.scalar_tensor_tensor(out=nbias[:], in0=mv[:, :, 0], scalar=-1.0, in1=rstd[:], op0=ALU.mult,
                                       op1=ALU.mult).then_inc(nb_ready, 1)

            def take_up(b, used):
                with dve.Fori(0, NJ // 2) as jj:
                    st.loop(jj, 16)
                    for q in range(2):
                        for t in range(NT):
                            j = 2 * jj + q
                            s, g = v[:, t, bass.ds(j * CW, CW)], sgn[:, t, bass.ds(j * CW, CW)]
                            st.done()
                            step(V.scalar_tensor_tensor(out=s, in0=s, scalar=tc[:, 0, t:t + 1], in1=s, op0=ALU.is_ge,
                                                        op1=ALU.mult))
                            st.done()
                            step(V.scalar_tensor_tensor(out=s, in0=g, scalar=-1.0, in1=s, op0=ALU.add, op1=ALU.mult))
                            st.done()
                            if t < NT - 1:
                                dve.wait_ge(u_done, 3 * NJ * b + 6 * jj + 3 * q + t + 1)
                            else:
                                dve.wait_ge(pe_used, used + 8 * jj + 4 * q + 4)
                            V.tensor_tensor(s, banks[4 * q + t][:, 0:CW], s, ALU.mult).then_inc(u_freed, 1)
                    st.end(16, NJ // 2)

            def turned(b):
                for c in range(NC):
                    rows = P if c < NC - 1 else LASTC
                    dve.wait_ge(t_hi, NC * b + c + 1)
                    V.tensor_tensor(hTl[0:rows, c, :], banks[c % 8][0:rows, :], hTh[0:rows, c, :].bitcast(F32),
                                    ALU.subtract).then_inc(t_lo, 1)

            def one(b):
                take_gate(b)
                search(b)

            n0 = st.n
            one(0)
            es.base, es.n = EXACT, 0
            take_up(0, NG)
            turned(0)
            per = st.n - n0 + 3 * NT
            with dve.Fori(1, NB) as b:
                st.loop(b - 1, per)
                es.loop(b - 1, EXACT)
                one(b)
                es.end(EXACT, NB - 1)
                used = used_base(b, False)
                take_down(b - 1, used + NG)
                take_up(b, used + NG + ND)
                turned(b)
                st.end(per, NB - 1)
            take_down(NB - 1, used_base(NB, False))
            dve.wait_ge(small_in, 16 * 9)
            A2 = [(slice(0, P), slice(0, CQ - 1)), (slice(0, LASTQ), slice(CQ - 1, CQ))]
            for p_, c_ in A2:
                step(V.tensor_copy(a2s[p_, :, c_, 0:R], a2raw[p_, :, c_, :]))
            st.done()
            for p_, c_ in A2:
                for q in range(Q4):
                    V.tensor_tensor(a2s[p_, q, c_, R:2 * R], a2raw[p_, q, c_, :], a2s[p_, q, c_, 0:R].bitcast(F32),
                                    ALU.subtract).then_inc(a_ready, 1)
            def fold_x(b, t):
                dve.wait_ge(x1t_ready, 2 * (NT * b + t + 1))
                if t == 0 and not (isinstance(b, int) and b == 0):
                    dve.wait_ge(uu_done, STEPS * b)
                st.done()
                V.tensor_reduce(xf[:], x1T[:, :, :].rearrange("p (q h) t -> p h t q", q=Q4), AX.X, ALU.add)\
                    .then_inc(l_fold, 1)
                dve.wait_ge(l_fold, NT * b + t + 1)
                tt = slice(t * P, (t + 1) * P)
                step(V.tensor_copy(xsh[:, :, tt], xf[:]))
                st.done()
                step(V.tensor_tensor(xsl[:, :, tt], xf[:], xsh[:, :, tt].bitcast(F32), ALU.subtract))

            def low_rank_x(b):
                dve.wait_ge(t1_done, NT * (b + 1))
                n = 2 * R
                step(V.tensor_copy(th[0:n, :], banks[7][0:n, :]))
                st.done()
                step(V.tensor_tensor(tl[0:n, :], banks[7][0:n, :], th[0:n, :].bitcast(F32), ALU.subtract))
                st.done()
                for i, dst in enumerate((lg, lu)):
                    for p0, src in ((0, th), (32, tl), (64, th)):
                        step(V.tensor_scalar(dst[p0:p0 + n, :], src[0:n, :].bitcast(F32), keep[0:n, i:i + 1], None,
                                             ALU.mult))
                st.done()
                dve.sem_inc(l_ready, 1)

            def steps_2(b):
                for m in range(STEPS):
                    c, q = m // Q4, m % Q4
                    rows = rows_of(c)
                    dve.wait_ge(uu_done, STEPS * b + m + 1)
                    dve.wait_ge(s_done, STEPS * b + m + 1)
                    if m >= 2:
                        dve.wait_ge(hl_done, STEPS * b + m - 1)
                    st.done()
                    V.tensor_tensor(h2[0:rows, m % 2, :], banks[2 * (m % 2) + 1][0:rows, :], sg[0:rows, m % 2, :],
                                    ALU.mult).then_inc(h_done, 1)
                    dve.wait_ge(h_done, STEPS * b + m + 1)
                    if q == 1:
                        if c:
                            dve.wait_ge(ql_done, CQ * b + c)
                        step(V.tensor_tensor(fold[0:rows, :], h2[0:rows, 0, :], h2[0:rows, 1, :], ALU.add))
                    elif q > 1:
                        st.done()
                        ins = V.tensor_tensor(fold[0:rows, :], fold[0:rows, :], h2[0:rows, m % 2, :], ALU.add)
                        if q == 3:
                            ins.then_inc(f_done, 1)
                            dve.wait_ge(f_done, CQ * b + c + 1)
                        else:
                            step(ins)

            def low_rank_h(b):
                n = 2 * R
                dve.wait_ge(t2_done, STEPS * (b + 1))
                step(V.tensor_copy(t2s[0:n, :], banks[4][0:n, :]))
                step(V.tensor_copy(t2s[64:64 + n, :], banks[4][0:n, :]))
                st.done()
                V.tensor_tensor(t2s[32:32 + n, :], banks[4][0:n, :], t2s[0:n, :].bitcast(F32), ALU.subtract)\
                    .then_inc(t2_ready, 1)

            def take_out(b, t):
                if t == 0:
                    dve.wait_ge(y_in, 16 * (b + 1))
                for n in range(2):
                    dve.wait_ge(e_done, 2 * NT * b + 2 * t + n + 1)
                    s = y[:, t, n * 512:(n + 1) * 512]
                    V.tensor_tensor(s, banks[2 * (t % 2) + n][:, :], s, ALU.add).then_inc(e_evac, 1)

            dve.wait_ge(keep_ready, 5)
            for t in range(NT):
                fold_x(0, t)
            low_rank_x(0)
            dve.wait_ge(b_ready, 2)
            V.scalar_tensor_tensor(out=b13[64:LR, :], in0=braw[64:LR, 0:I], scalar=LORA,
                                   in1=b13[64:LR, :].bitcast(F32), op0=ALU.mult, op1=ALU.subtract).then_inc(b_ready, 1)
            V.scalar_tensor_tensor(out=b2s[64:LR, :], in0=braw[64:LR, I:I + H], scalar=LORA,
                                   in1=b2s[64:LR, :].bitcast(F32), op0=ALU.mult, op1=ALU.subtract).then_inc(b_ready, 1)
            n0 = st.n
            SB = 2 * 6 + 2 + 8 + 2 * NT + 3 * NT
            with dve.Fori(0, NB - 1) as b:
                st.loop(b, SB)
                steps_2(b)
                low_rank_h(b)
                for t in range(NT):
                    fold_x(b + 1, t)
                    take_out(b, t)
                dve.wait_ge(e_evac, 2 * NT * (b + 1))
                low_rank_x(b + 1)
                norm_sums(NB + b, None)
                st.end(SB, NB - 1)
            steps_2(NB - 1)
            low_rank_h(NB - 1)
            for t in range(NT):
                take_out(NB - 1, t)
            dve.wait_ge(e_evac, 2 * NT * NB)
            norm_sums(2 * NB - 1, None)

        @block.tensor
        def _(pe):
            pe.wait_ge(consts, 2)

            def three(dst, ah, al, bh, bl, start, stop):
                nc.tensor.matmul(dst, ah, bh, start=start, stop=False)
                nc.tensor.matmul(dst, ah, bl, start=False, stop=False)
                return nc.tensor.matmul(dst, al, bh, start=False, stop=stop)

            def gate_up(b, base, done, freed, takes_x=False):
                chunks(b, base, 0, (0,), done, freed, takes_x)
                chunks(b, base, 0, (1,), done, freed)
                with pe.Fori(1, NJ // 2) as jj:
                    chunks(b, base, jj, (0, 1), done, freed)

            def chunks(b, base, jj, qs, done, freed, takes_x=False):
                if True:
                    for q in qs:
                        for i in range(4):
                            pe.wait_ge(lo_done, base + 8 * jj + 4 * q + i + 1)
                            if takes_x:
                                pe.wait_ge(x_lo, KH * b + 2 * i + 2)
                            for k in (2 * i, 2 * i + 1):
                                w = slice(k * CW, (k + 1) * CW)
                                for t in range(NT):
                                    if k == 0:
                                        pe.wait_ge(freed, 4 * NJ * b + 8 * jj + 4 * q + t + 1)
                                    tt = slice(t * P, (t + 1) * P)
                                    ins = three(banks[4 * q + t][:, 0:CW], xTh[:, k, tt], xTl[:, k, tt], wh[:, w],
                                                wl[:, w], k == 0, k == KH - 1)
                                    if k == KH - 1 and t < NT - 1:
                                        ins.then_inc(done, 1)
                            ins.then_inc(pe_used, 1)

            def down(b1, base):
                for c in range(NC):
                    rows = P if c < NC - 1 else LASTC
                    for n in range(2):
                        d = 2 * c + n
                        pe.wait_ge(lo_done, base + d + 1)
                        w = slice((d % 4) * 512, (d % 4 + 1) * 512)
                        for t in range(NT):
                            tt = slice(t * P, (t + 1) * P)
                            ins = three(banks[2 * t + n][:, :], hTh[0:rows, c, tt], hTl[0:rows, c, tt],
                                        wh[0:rows, w], wl[0:rows, w], c == 0, c == NC - 1)
                            if c == NC - 1 and t < NT - 1:
                                ins.then_inc(d_done, 1)
                        ins.then_inc(pe_used, 1)

            def turn(b):
                pe.wait_ge(u_freed, 8 + 4 * NJ * (b + 1))
                for c in range(NC):
                    rows = P if c < NC - 1 else LASTC
                    if c >= 8:
                        pe.wait_ge(t_lo, NC * b + c - 8 + 1)
                        pe.sem_inc(passed_pe, 1)
                    for t in range(NT):
                        ins = nc.tensor.transpose(banks[c % 8][0:rows, t * P:(t + 1) * P],
                                                  v[:, t, c * P:c * P + rows], ident[:, :])
                    ins.then_inc(t_done, 1)

            gate_up(0, 0, g_done, g_freed, True)
            pe.wait_ge(g_freed, 8 + 4 * NJ)
            gate_up(0, NG, u_done, u_freed)
            turn(0)
            with pe.Fori(1, NB) as b:
                base = used_base(b, False)
                pe.wait_ge(t_lo, NC * b)
                pe.sem_inc(passed_pe, 1)
                gate_up(b, base, g_done, g_freed, True)
                pe.wait_ge(g_freed, 8 + 4 * NJ * (b + 1))
                pe.sem_inc(passed_pe, 1)
                down(b - 1, base + NG)
                pe.wait_ge(d_evac, 8 * b)
                pe.sem_inc(passed_pe, 1)
                gate_up(b, base + NG + ND, u_done, u_freed)
                turn(b)
            pe.wait_ge(t_lo, NC * NB)
            down(NB - 1, used_base(NB, False))

            def turn_x(b, t):
                pe.wait_ge(xa_in[t % 2], 16 * (2 * b + t // 2 + 1))
                if not (isinstance(b, int) and b == 0 and t == 0):
                    pe.wait_ge(x1t_ready, 2 * (NT * b + t))
                for k in range(KH):
                    ins = nc.tensor.transpose(banks[5 + k // 4][:, (k % 4) * P:(k % 4 + 1) * P],
                                              xa[:, t % 2, k * P:(k + 1) * P], ident[:, :])
                ins.then_inc(x1t_done, 1)

            def low_rank(b, t):
                pe.wait_ge(x1t_ready, 2 * (NT * b + t + 1))
                if t == 0:
                    pe.sem_inc(passed_pe, 1)
                for k in range(KH):
                    ins = nc.tensor.matmul(banks[7][0:2 * R, t * P:(t + 1) * P], a13s[:, k, :], x1T[:, k, :],
                                           start=k == 0, stop=k == KH - 1)
                ins.then_inc(t1_done, 1)

            def steps_2(b):
                base = USED2 + NW13 * b
                pe.wait_ge(l_ready, b + 1)

                def low_h(m, frees):
                    c, q = m // Q4, m % Q4
                    rows = rows_of(c)
                    pe.wait_ge(hl_done, STEPS * b + m + 1)
                    pe.sem_inc(passed_pe, 1)
                    w = a2s[0:rows, q, c, :]
                    i1 = nc.tensor.matmul(banks[4][0:2 * R, :], w, h2h[0:rows, m % 2, :], start=m == 0, stop=False)
                    if frees:
                        i1.then_inc(pe_used, 4)
                    nc.tensor.matmul(banks[4][0:2 * R, :], w, h2l[0:rows, m % 2, :], start=False,
                                     stop=m == STEPS - 1).then_inc(t2_done, 1)

                for m in range(STEPS):
                    c, q = m // Q4, m % Q4
                    rows = rows_of(c)
                    if q == 0:
                        pe.wait_ge(lo_done, base + 4 * c + 4)
                        pe.sem_inc(passed_pe, 1)
                    for i, (low_x, done) in enumerate(((lg, gg_done), (lu, uu_done))):
                        dst = banks[2 * (m % 2) + i][0:rows, :]
                        if m >= 2:
                            pe.wait_ge((s_done, h_done)[i], STEPS * b + m - 1)
                            pe.sem_inc(passed_pe, 1)
                        for k in range(KQ):
                            s, mm = (c % 2) * 4 + 2 * i + k, slice(q * rows, (q + 1) * rows)
                            three(dst, w13h[:, s, mm], w13l[:, s, mm], xsh[:, k, :], xsl[:, k, :], k == 0, False)
                        mm = slice(q * IQ + c * P, q * IQ + c * P + rows)
                        nc.tensor.matmul(dst, b13[0:LR, mm], low_x[0:LR, :], start=False, stop=True).then_inc(done, 1)
                    if m >= 2:
                        low_h(m - 2, q == 3)
                low_h(STEPS - 2, False)
                low_h(STEPS - 1, False)

            def down_2(b, t):
                if t == 0:
                    pe.wait_ge(ql_done, CQ * (b + 1))
                    pe.sem_inc(passed_pe, 1)
                elif t >= 2:
                    pe.wait_ge(e_evac, 2 * NT * b + 2 * (t - 1))
                    pe.sem_inc(passed_pe, 1)
                tt = slice(t * P, (t + 1) * P)
                for n in range(2):
                    dst, w = banks[2 * (t % 2) + n][:, :], slice(n * 512, (n + 1) * 512)
                    for c in range(CQ):
                        rows = rows_of(c)
                        three(dst, hqh[0:rows, c, tt], hql[0:rows, c, tt], w2h[0:rows, c, w], w2l[0:rows, c, w],
                              c == 0, False)
                    if t == 0 and n == 0:
                        pe.wait_ge(t2_ready, b + 1)
                        pe.sem_inc(passed_pe, 1)
                    nc.tensor.matmul(dst, t2s[0:LR, tt], b2s[0:LR, w], start=False, stop=True).then_inc(e_done, 1)

            pe.wait_ge(small_in, 16 * 9)
            pe.wait_ge(d_evac, 8 * NB)
            for t in range(NT):
                turn_x(0, t)
                low_rank(0, t)
            pe.wait_ge(b_ready, 4)
            pe.wait_ge(a_ready, 2 * Q4)
            pe.wait_ge(keep_ready, 5)
            pe.wait_ge(w2_lo, NW2)
            with pe.Fori(0, NB - 1) as b:
                steps_2(b)
                for t in range(NT):
                    turn_x(b + 1, t)
                    down_2(b, t)
                    low_rank(b + 1, t)
            steps_2(NB - 1)
            for t in range(NT):
                down_2(NB - 1, t)


def kernel(L0_attn_x, L0_attn_w_gate, L0_attn_w_up, L0_attn_w_down, L0_ffn_w1q, L0_ffn_a1, L0_ffn_b1, L0_ffn_w3q,
           L0_ffn_a3, L0_ffn_b3, L0_ffn_w2q, L0_ffn_a2, L0_ffn_b2):
    import numpy as np
    import concourse.bacc as bacc
    from concourse.bass_utils import run_bass_kernel_spmd as run

    x = np.asarray(L0_attn_x).reshape(TOK, H)
    xT = np.ascontiguousarray(x.reshape(NB, TB, KH, P).transpose(0, 3, 2, 1)).reshape(NB, P, KH * TB)
    xtok = np.ascontiguousarray(x.reshape(NB, NT, P, H).transpose(0, 2, 1, 3))

    def by_chunk(w):
        w = np.asarray(w).reshape(NJ, CW, KH, P)
        return np.ascontiguousarray(w.transpose(0, 3, 2, 1)).reshape(NJ, P, KH * CW)

    w = np.stack([np.asarray(L0_ffn_w1q), np.asarray(L0_ffn_w3q)]).reshape(2, Q4, IQ, KQ, P)
    full = w[:, :, :(CQ - 1) * P].reshape(2, Q4, CQ - 1, P, KQ, P)
    w13 = np.ascontiguousarray(full.transpose(2, 0, 4, 5, 1, 3)).reshape(CQ - 1, 2, KQ, P, Q4 * P)
    w13t = np.ascontiguousarray(w[:, :, (CQ - 1) * P:].transpose(0, 3, 4, 1, 2)).reshape(2, KQ, P, Q4 * LASTQ)
    a13 = np.concatenate([np.asarray(L0_ffn_a1), np.asarray(L0_ffn_a3)]).reshape(2 * R, KH, P)

    def turned(a):
        return np.ascontiguousarray(np.asarray(a).T)

    arrays = {"in_xT": xT, "in_xtok": xtok, "in_wg": by_chunk(L0_attn_w_gate), "in_wu": by_chunk(L0_attn_w_up),
              "in_wd": turned(L0_attn_w_down), "in_w13": w13, "in_w13t": w13t, "in_w2": turned(L0_ffn_w2q),
              "in_a13": np.ascontiguousarray(a13.transpose(2, 1, 0)), "in_a2": turned(L0_ffn_a2),
              "in_b1": turned(L0_ffn_b1), "in_b3": turned(L0_ffn_b3), "in_b2": turned(L0_ffn_b2)}
    nc = bacc.Bacc("TRN2", target_bir_lowering=False, num_devices=1)
    aps = [nc.dram_tensor(n, a.shape, F32, kind="ExternalInput").ap() for n, a in arrays.items()]
    o = nc.dram_tensor("out_y", (NB, P, NT, H), F32, kind="ExternalOutput").ap()
    program(nc, *aps, o)
    r = run(nc, [arrays], core_ids=[0])
    return np.ascontiguousarray(r.results[0]["out_y"].transpose(0, 2, 1, 3)).reshape(2, 1024, 1024)
```

```python
from contextlib import ExitStack

import concourse.bass as bass
from concourse import mybir

F32 = mybir.dt.float32
F32R = mybir.dt.float32r
I8 = mybir.dt.int8
I32 = mybir.dt.int32
ALU = mybir.AluOpType
ACT = mybir.ActivationFunctionType
AX = mybir.AxisListType
RMAX = bass.bass_isa.ReduceOp.max

P = 128
TOK, H, I = 2048, 1024, 2752
TB = 512
NB = TOK // TB
NT = TB // P
KH = H // P
CW = 344
NJ = I // CW
KEEP_FROM = I // 2
NC = -(-I // P)
LASTC = I - (NC - 1) * P
SETS = [[c for c in range(NC) if j * CW < min(P * (c + 1), I) <= (j + 1) * CW] for j in range(NJ)]
ROUNDS = 6
BIG = 1.0e30
EPS = 1e-5

NG, ND, NU = NJ * KH // 2, 2 * NC, NJ * KH // 2
USED0, USEDB = NG + NU, NG + ND + NU

Q4 = 4
HQ = H // Q4
KQ = HQ // P
IQ = I // Q4
CQ = -(-IQ // P)
LASTQ = IQ - (CQ - 1) * P
HALF = P // 2
PAIR = HALF + LASTQ
R = 2
LORA = 0.5
STEPS = (CQ - 1) * Q4 + Q4 // 2
IB = (CQ - 1) * Q4 * P + Q4 // 2 * PAIR
LR = 96
NW2, NW13 = 2 * CQ, 4 * CQ
USED2 = USED0 + USEDB * (NB - 1) + ND


def rows_in(c):
    return P if c < NC - 1 else LASTC


def rows_of(c):
    return P if c < CQ - 1 else PAIR


def steps_of(c):
    return Q4 if c < CQ - 1 else Q4 // 2


def place(m):
    c = m // Q4
    return c, m - Q4 * c, rows_of(c)


class Steps:

    def __init__(self, eng, sem):
        self.eng, self.sem, self.base, self.n, self.outer = eng, sem, 0, 0, []

    def mark(self, ins):
        ins.then_inc(self.sem, 1)
        self.n += 1
        return self

    def done(self):
        self.eng.wait_ge(self.sem, self.base + self.n)

    def done_apart(self, passed):
        self.done()
        self.eng.sem_inc(passed, 1)

    def loop(self, i, per):
        self.outer.append((self.base, self.n))
        self.base, self.n = self.base + self.n + i * per, 0

    def end(self, per, count):
        assert self.n == per, (self.n, per)
        base, n = self.outer.pop()
        self.base, self.n = base, n + per * count


def program(nc, xT, xtok, wg, wu, wd, w13, w2, a13, a2, b1, b3, b2, out):
    x1 = nc.dram_tensor("x1", (NB, P, NT, H), F32, kind="Internal").ap()
    with ExitStack() as ctx:
        def sem(name):
            return ctx.enter_context(nc.semaphore(name))

        def bank(name):
            return ctx.enter_context(nc.psum_tensor(name, [P, 512], F32))

        room = 212600
        arena = ctx.enter_context(nc.sbuf_tensor("arena", [P, room], I8))
        start = nc.sbuf_base - room if nc.sbuf_base >= room else 0
        at = {"next": start}

        def sb(name, shape, dt, size, offset=None):
            n = size
            for d in shape[1:]:
                n *= d
            o = at["next"] if offset is None else offset
            if offset is None:
                at["next"] = -(-(o + n) // 32) * 32
                assert at["next"] <= start + room, (name, at["next"] - start)
            at[name] = o
            return nc.alloc_sbuf_tensor_at(name, shape, dt, offset=o)

        v = sb("v", [P, NT, I], F32, 4)
        hTh = sb("hTh", [P, NC, TB], F32R, 4)
        hTl = sb("hTl", [P, NC, TB], F32R, 4)
        s0 = sb("s0", [P, NJ, NT, CW], F32, 4, offset=at["hTh"])
        w0 = sb("w0", [P, NJ, NT, CW], F32, 4, offset=at["hTl"])
        xTh = sb("xTh", [P, KH, TB], F32R, 4)
        xTl = sb("xTl", [P, KH, TB], F32R, 4)
        wh = sb("wh", [P, 8 * CW], F32R, 4)
        wl = sb("wl", [P, 8 * CW], F32R, 4)
        x_in_place = sb("x_in_place", [P, KH, TB], F32, 4, offset=at["xTl"])
        w_in_place = sb("w_in_place", [P, 8 * CW], F32, 4, offset=at["wl"])
        sgn = sb("sgn", [P, NT, I], I8, 1)
        junkd = sb("junkd", [P, I], I8, 1)
        junka = sb("junka", [P, I // 2], I8, 1)
        ident = sb("ident", [P, P], F32, 4)
        YC = NC - NT * H // TB
        y = sb("y", [P, NT, H], F32, 4, offset=at["hTh"] + YC * TB * 4)
        scr = sb("scr", [P, I // 2], F32, 4)
        mags = sb("mags", [P, NT, NJ], F32, 4)
        tc = sb("tc", [P, 2, NT], F32, 4)
        lc = sb("lc", [P, 2, NT], F32, 4)
        hc = sb("hc", [P, 2, NT], F32, 4)
        le = sb("le", [P, 2, NT], F32, 4)
        qa = sb("qa", [P, 2, NT], F32, 4)
        qb = sb("qb", [P, 2, NT], F32, 4)
        negt = sb("negt", [P, NT], F32, 4)
        ssum = sb("ssum", [P, 2, 2], F32, 4)
        sadd = sb("sadd", [P, 2], F32, 4)
        cand = sb("cand", [P, 16], F32, 4)
        top8 = sb("top8", [P, 8], F32, 4)
        pick = sb("pick", [P, 8], F32, 4)
        iota8 = sb("iota8", [P, 8], F32, 4)
        bad = sb("bad", [P, 1], F32, 4)
        flag = sb("flag", [P, 1], F32, 4)
        bit = sb("bit", [P, NT], I32, 4)
        taken = sb("taken", [P, NT], I32, 4)
        carry = sb("carry", [P, 1], F32, 4)
        stats = sb("stats", [P, NT, 2, 6], F32, 4)
        mv = sb("mv", [P, NT, 2], F32, 4)
        ve = sb("ve", [P, NT], F32, 4)
        mhalf = sb("mhalf", [P, NT], F32, 4)
        rstd = sb("rstd", [P, NT], F32, 4)
        nbias = sb("nbias", [P, NT], F32, 4)

        over = {"at": at["v"]}

        def put(name, shape, dt):
            n = 4
            for d in shape[1:]:
                n *= d
            o = over["at"]
            over["at"] = -(-(o + n) // 32) * 32
            return sb(name, shape, dt, 4, offset=o)

        w2h = put("w2h", [P, CQ, H], F32R)
        b13 = put("b13", [P, IB], F32R)
        b2s = put("b2s", [P, H], F32R)
        a2s = put("a2s", [P, STEPS, 2 * R], F32R)
        a2raw = put("a2raw", [P, STEPS, R], F32)
        a13s = put("a13s", [P, KH, 2 * R], F32)
        keep = put("keep", [P, 2], F32)
        t2s = put("t2s", [P, TB], F32R)
        assert over["at"] <= at["hTh"]
        over["at"] = at["xTh"]
        w2l = put("w2l", [P, CQ, H], F32R)
        w2_in_place = sb("w2_in_place", [P, CQ, H], F32, 4, offset=at["w2l"])
        xa = put("xa", [P, 2, H], F32)
        assert over["at"] <= at["wh"]
        over["at"] = at["hTh"]
        x1T = put("x1T", [P, KH, P], F32)
        xf = put("xf", [P, KQ, P], F32)
        th = put("th", [P, TB], F32R)
        tl = put("tl", [P, TB], F32R)
        w13h = put("w13h", [P, 8, 512], F32R)
        lg = put("lg", [P, TB], F32R)
        assert over["at"] <= at["y"]
        over["at"] = at["hTl"]
        xsh = put("xsh", [P, KQ, TB], F32R)
        xsl = put("xsl", [P, KQ, TB], F32R)
        sg = put("sg", [P, 2, TB], F32)
        h2 = put("h2", [P, 2, TB], F32)
        h2h = put("h2h", [P, 2, TB], F32R)
        h2l = put("h2l", [P, 2, TB], F32R)
        fold = put("fold", [P, TB], F32)
        lu = put("lu", [P, TB], F32R)
        w13l = put("w13l", [P, 8, 512], F32R)
        assert over["at"] <= at["xTh"]
        w13_in_place = sb("w13_in_place", [P, 8, 512], F32, 4, offset=at["w13l"])
        over["at"] = at["w13l"]
        braw = put("braw", [P, IB + H], F32)
        assert over["at"] <= at["xTh"]

        def down_done_with(name, h):
            return USED2 - ND + 2 * (NC - (at[name] - at[h]) // (TB * 4))
        over["at"] = at["wh"]
        hqh = put("hqh", [P, CQ, TB], F32R)
        hql = put("hql", [P, CQ, TB], F32R)
        assert over["at"] <= at["junkd"]

        banks = [bank(f"bank{i}") for i in range(8)]

        raw_in = [sem(f"raw_in{i}") for i in range(4)]
        x_raw = [sem(f"x_raw{i}") for i in range(KH)]
        x_hi, x_lo = sem("x_hi"), sem("x_lo")
        w2_raw = [sem(f"w2_raw{i}") for i in range(NW2)]
        w2_hi, w2_lo = sem("w2_hi"), sem("w2_lo")
        hi_done, lo_done, pe_used = sem("hi_done"), sem("lo_done"), sem("pe_used")
        g_done, g_freed = sem("g_done"), sem("g_freed")
        u0_copied, w0_ready = sem("u0_copied"), sem("w0_ready")
        u_done, u_freed = sem("u_done"), sem("u_freed")
        t_done, t_hi, t_lo = sem("t_done"), sem("t_hi"), sem("t_lo")
        d_done, d_evac = sem("d_done"), sem("d_evac")
        probe, signs = sem("probe"), sem("signs")
        bad_ready, flag_ready = sem("bad_ready"), sem("flag_ready")
        x_in, ve_ready, rstd_ready, nb_ready, norm_done, x1_out = (
            sem("x_in"), sem("ve_ready"), sem("rstd_ready"), sem("nb_ready"), sem("norm_done"), sem("x1_out"))
        xa_in = [sem(f"xa_in{i}") for i in range(2)]
        small_in, b_zero, b_in, b_ready, a_ready, keep_ready = (
            sem("small_in"), sem("b_zero"), sem("b_in"), sem("b_ready"), sem("a_ready"), sem("keep_ready"))
        l_fold = sem("l_fold")
        x1t_done, x1t_ready, t1_done, l_ready = sem("x1t_done"), sem("x1t_ready"), sem("t1_done"), sem("l_ready")
        gg_done, uu_done, s_done, h_done, f_done = (
            sem("gg_done"), sem("uu_done"), sem("s_done"), sem("h_done"), sem("f_done"))
        hh_done, hl_done, t2_done, t2_ready = sem("hh_done"), sem("hl_done"), sem("t2_done"), sem("t2_ready")
        qh_done, ql_done, e_done, e_evac, y_in, out_done = (
            sem("qh_done"), sem("ql_done"), sem("e_done"), sem("e_evac"), sem("y_in"), sem("out_done"))
        passed_dve, passed_pool, passed_pe, passed_sp = (
            sem("passed_dve"), sem("passed_pool"), sem("passed_pe"), sem("passed_sp"))
        exact_s = sem("exact_s")
        consts, dve_s, act_s, pool_s = sem("consts"), sem("dve_s"), sem("act_s"), sem("pool_s")

        block = ctx.enter_context(nc.Block())
        FRONT, BACK = slice(0, NT - 1), slice(NT - 1, NT)
        LAST_D = USED2 - ND

        def used_base(b, first):
            return 0 if first else USED0 + USEDB * (b - 1)

        def landed(base, i):
            return 4 * base + 16 * (i // 4) + 16

        def free_d(i, base):
            return base + i - 4 + 1

        def free_u(i, base, first):
            if first or i >= 4:
                return base + i - 4 + 1
            return base - 4 + min(i + 1, 3) + 1

        @block.sync
        def _(sp):
            def load(slot, dst, src, free):
                if free is not None:
                    sp.wait_ge(pe_used, free)
                sp.sem_inc(passed_sp, 1)
                sp.dma_start(dst, src).then_inc(raw_in[slot], 16)

            def load_gu_piece(w, chunk, i, free):
                c, s = i % 4 * 2 * CW, slice(i % 4 * 2 * CW, (i % 4 + 1) * 2 * CW)
                load(i % 4, w_in_place[:, s],
                     w[bass.ds(chunk, 1), :, c:c + 2 * CW].rearrange("o p n -> (o p) n"), free)

            def load_head(b, base, first):
                for i in range(4):
                    for k in (2 * i, 2 * i + 1):
                        if not first:
                            sp.wait_ge(pe_used, base - 4 + i + 1)
                        sp.sem_inc(passed_sp, 1)
                        sp.dma_start(x_in_place[:, k, :], xT[bass.ds(b, 1), :, k * TB:(k + 1) * TB]
                                     .rearrange("o p n -> (o p) n")).then_inc(x_raw[k], 16)
                    load_gu_piece(wg, 0, i, None if first else base - 4 + i + 1)

            def load_gu(w, base):
                with sp.Fori(0, NJ // 2 - 1) as jj:
                    for i in range(4, 12):
                        load_gu_piece(w, 2 * jj + i // 4, i, base + 8 * jj + i - 3)
                for i in range(NG - 4, NG):
                    load_gu_piece(w, NJ - 1, i, base + i - 3)

            def load_u(base, first):
                for i in range(4):
                    load_gu_piece(wu, 0, i, free_u(i, base, first))
                load_gu(wu, base)

            def load_d(base, meanwhile=None):
                def piece(c, d, free, rows=P):
                    s = slice(d % 4 * 512, (d % 4 + 1) * 512)
                    load(d % 4, w_in_place[0:rows, s], wd[bass.ds(c * P, rows), d % 2 * 512:(d % 2 + 1) * 512], free)
                for d in range(4):
                    piece(NC - 1 - d // 2, d, free_d(d, base), rows_in(NC - 1 - d // 2))
                if meanwhile is not None:
                    for d in range(4, ND):
                        if d in meanwhile:
                            meanwhile[d]()
                        piece(NC - 1 - d // 2, d, base + d - 3)
                    return
                with sp.Fori(1, ND // 4) as g:
                    for d in range(4):
                        piece(NC - 1 - d // 2 - 2 * g, d, base + 4 * g + d - 3)

            def x_tiles(b1, used):
                sp.wait_ge(pe_used, used)
                sp.sem_inc(passed_sp, 1)
                sp.dma_start(y[:, :, :], xtok[bass.ds(b1, 1), :, :, :].rearrange("o p t h -> (o p) t h"))\
                    .then_inc(x_in, 16)

            load_head(0, 0, True)
            load_gu(wg, 0)
            load_u(NG, True)
            with sp.Fori(1, NB) as b:
                base = used_base(b, False)
                load_head(b, base, False)
                load_gu(wg, base)
                load_d(base + NG)
                x_tiles(b - 1, base + NG + 16)
                load_u(base + NG + ND, False)

            def load_w2():
                for d in range(NW2):
                    rows = rows_of(d // 2)
                    sp.dma_start(w2_in_place[0:rows, d // 2, (d % 2) * 512:(d % 2 + 1) * 512],
                                 w2[d // 2, 0:rows, (d % 2) * 512:(d % 2 + 1) * 512]).then_inc(w2_raw[d], 16)

            def load_small():
                sp.wait_ge(t_done, NC * NB)
                sp.dma_start(a13s[:, :, :], a13).then_inc(small_in, 16)
                sp.dma_start(a2raw[:, :, :], a2).then_inc(small_in, 16)

            def load_b():
                sp.wait_ge(b_zero, 1)
                for g in range(3):
                    for i, (src, c0) in enumerate(((b1, 0), (b3, 0), (b2, IB), (b2, IB))):
                        r0 = 32 * g + R * (i % 2)
                        sp.dma_start(braw[r0:r0 + R, c0:c0 + src.shape[1]], src).then_inc(b_in, 16)

            def load_xa(b, tiles=range(NT)):
                sp.wait_ge(x1_out, 16 * NT * (b + 1))
                for t in tiles:
                    if t >= 2 or not (isinstance(b, int) and b == 0):
                        sp.sem_inc(passed_sp, 1)
                        sp.wait_ge(x1t_done, NT * b + t - 1)
                    sp.sem_inc(passed_sp, 1)
                    sp.dma_start(xa[:, t % 2, :], x1[bass.ds(b, 1), :, t, :].rearrange("o p h -> (o p) h"))\
                        .then_inc(xa_in[t % 2], 16)

            def load_13(b, chunks):
                base = USED2 + NW13 * b
                for c in chunks:
                    first = isinstance(b, int) and b == 0
                    for i in range(4):
                        w, k = i // 2, i % 2
                        s, m = (c % 2) * 4 + i, steps_of(c) * rows_of(c)
                        if first and c < 2:
                            if c == i == 0:
                                sp.wait_ge(b_ready, 4)
                                sp.wait_ge(pe_used, down_done_with("w13h", "hTh"))
                        else:
                            sp.wait_ge(pe_used, base + 4 * (c - 1))
                        sp.sem_inc(passed_sp, 1)
                        sp.wait_ge(hi_done, base + 4 * (c - 1) + i + 1)
                        sp.sem_inc(passed_sp, 1)
                        sp.dma_start(w13_in_place[:, s, 0:m], w13[c, w, k, :, 0:m])\
                            .then_inc(raw_in[i], 16)

            def load_y(b):
                sp.wait_ge(x1_out, 16 * NT * NB)
                if isinstance(b, int) and b == 0:
                    pass
                else:
                    sp.wait_ge(out_done, 16 * NT * b)
                sp.sem_inc(passed_sp, 1)
                sp.dma_start(y[:, :, :], x1[bass.ds(b, 1), :, :, :].rearrange("o p t h -> (o p) t h"))\
                    .then_inc(y_in, 16)

            load_d(LAST_D, {4: load_w2, 5: load_small, 6: lambda: load_xa(0, (0, 1)), 22: load_b,
                            24: lambda: x_tiles(NB - 1, LAST_D + 16)})
            load_13(0, (0, 1))
            load_xa(0, (2, 3))
            load_13(0, range(2, CQ))
            load_y(0)
            with sp.Fori(1, NB) as b:
                load_xa(b, (0, 1))
                load_13(b, (0,))
                load_xa(b, (2, 3))
                load_13(b, range(1, CQ))
                load_y(b)
            sp.wait_ge(out_done, 16 * NT * NB)

        @block.gpsimd
        def _(pool):
            nc.gpsimd.memset(ident[:], 0.0).then_inc(pool_s, 1)
            pool.wait_ge(pool_s, 1)
            nc.gpsimd.affine_select(out=ident[:], in_=ident[:], compare_op=ALU.not_equal, fill=1.0, base=0,
                                    pattern=[[-1, P]], channel_multiplier=1).then_inc(consts, 1)
            nc.gpsimd.iota(iota8[:], pattern=[[1, 8]], base=0, channel_multiplier=0,
                           allow_small_or_imprecise_dtypes=True).then_inc(consts, 1)
            nc.gpsimd.memset(mhalf[:], -0.5).then_inc(pool_s, 1)
            pool.wait_ge(pool_s, 2)

            def less(hi, lo, landed, done):
                nc.gpsimd.tensor_tensor(lo, landed, hi.bitcast(F32), ALU.subtract).then_inc(done, 1)

            def low(n, hi, lo, landed):
                pool.wait_ge(hi_done, n + 1)
                less(hi, lo, landed, lo_done)

            def low_gu_piece(n, i):
                s = slice((i % 4) * 2 * CW, (i % 4 + 1) * 2 * CW)
                low(n, wh[:, s], wl[:, s], w_in_place[:, s])

            def low_head(b, base):
                for i in range(4):
                    for k in (2 * i, 2 * i + 1):
                        pool.wait_ge(x_hi, KH * b + k + 1)
                        less(xTh[:, k, :], xTl[:, k, :], x_in_place[:, k, :], x_lo)
                    low_gu_piece(base + i, i)

            def low_gu(base, given=0):
                for i in range(given, 8):
                    low_gu_piece(base + i, i)
                with pool.Fori(1, NJ // 2) as jj:
                    for i in range(8):
                        low_gu_piece(base + 8 * jj + i, i)

            def low_d(base):
                def one(n, d, rows):
                    s = slice((d % 4) * 512, (d % 4 + 1) * 512)
                    low(n, wh[0:rows, s], wl[0:rows, s], w_in_place[0:rows, s])
                for d in range(4):
                    one(base + d, d, rows_in(NC - 1 - d // 2))
                with pool.Fori(1, ND // 4) as g:
                    for d in range(4):
                        one(base + 4 * g + d, d, P)

            def flagged(b):
                pool.wait_ge(bad_ready, b + 1)
                pool.sem_inc(passed_pool, 1)
                nc.gpsimd.partition_all_reduce(flag[:, 0:1], bad[:, 0:1], P, RMAX).then_inc(flag_ready, 1)

            def inv_std(n, whole=slice(0, NT)):
                pool.wait_ge(ve_ready, n + 1)
                nc.gpsimd.tensor_tensor(rstd[:, whole], ve[:, whole], mhalf[:, whole], ALU.pow).then_inc(rstd_ready, 1)

            low_head(0, 0)
            low_gu(0, 4)
            for i in range(8):
                low_gu_piece(NG + i, i)
            for j in range(NJ):
                for t in range(NT):
                    if j < NJ - 2:
                        low_gu_piece(NG + 4 * (j + 2) + t, t)
                    w = w0[:, j, t, :]
                    pool.wait_ge(u0_copied, 4 * j + t + 1)
                    nc.gpsimd.tensor_tensor(w, w, s0[:, j, t, :], ALU.mult).then_inc(w0_ready, 1)
            flagged(0)
            with pool.Fori(1, NB) as b:
                base = used_base(b, False)
                low_head(b, base)
                low_gu(base, 4)
                low_d(base + NG)
                flagged(b)
                base_u = base + NG + ND
                for i in range(4):
                    low_gu_piece(base_u + i, i)
                inv_std(b - 1)
                low_gu(base_u, 4)
            for d in range(ND):
                sl = slice((d % 4) * 512, (d % 4 + 1) * 512)
                rows = rows_in(NC - 1 - d // 2)
                low(LAST_D + d, wh[0:rows, sl], wl[0:rows, sl], w_in_place[0:rows, sl])
                if d == 4:
                    pool.wait_ge(t_done, NC * NB)
                    nc.gpsimd.memset(keep[:], 1.0).then_inc(pool_s, 1)
                    pool.wait_ge(pool_s, 3)
                    nc.gpsimd.affine_select(out=keep[:, 0:1], in_=keep[:, 0:1], compare_op=ALU.is_ge, fill=0.0,
                                            base=R - 1, pattern=[[0, 1]], channel_multiplier=-1).then_inc(keep_ready, 1)
                    nc.gpsimd.affine_select(out=keep[:, 1:2], in_=keep[:, 1:2], compare_op=ALU.is_ge, fill=0.0,
                                            base=-R, pattern=[[0, 1]], channel_multiplier=1).then_inc(keep_ready, 1)
                    nc.gpsimd.memset(t2s[0:LR, :].bitcast(F32), 0.0).then_inc(keep_ready, 1)
                if d == 19:
                    pool.wait_ge(pe_used, down_done_with("braw", "hTl"))
                    nc.gpsimd.memset(braw[0:LR, :], 0.0).then_inc(b_zero, 1)
                if d == 28:
                    pool.wait_ge(pe_used, max(down_done_with("lg", "hTh"), down_done_with("lu", "hTl")))
                    nc.gpsimd.memset(lg[0:LR, :].bitcast(F32), 0.0).then_inc(keep_ready, 1)
                    nc.gpsimd.memset(lu[0:LR, :].bitcast(F32), 0.0).then_inc(keep_ready, 1)
                if d >= ND - NW2:
                    e = d - (ND - NW2)
                    c, sl, rows = e // 2, slice((e % 2) * 512, (e % 2 + 1) * 512), rows_of(e // 2)
                    pool.wait_ge(w2_hi, e + 1)
                    less(w2h[0:rows, c, sl], w2l[0:rows, c, sl], w2_in_place[0:rows, c, sl], w2_lo)

            def low_13(b, c, i):
                s, m = (c % 2) * 4 + i, steps_of(c) * rows_of(c)
                low(USED2 + NW13 * b + 4 * c + i, w13h[:, s, 0:m], w13l[:, s, 0:m], w13_in_place[:, s, 0:m])

            def steps_2(b, last):
                def low_h(m):
                    rows = place(m)[2]
                    pool.wait_ge(hh_done, STEPS * b + m + 1)
                    nc.gpsimd.tensor_tensor(h2l[0:rows, m % 2, :], h2[0:rows, m % 2, :],
                                            h2h[0:rows, m % 2, :].bitcast(F32), ALU.subtract).then_inc(hl_done, 1)

                def low_q(c):
                    rows = rows_of(c)
                    pool.wait_ge(qh_done, CQ * b + c + 1)
                    nc.gpsimd.tensor_tensor(hql[0:rows, c, :], fold[0:rows, :], hqh[0:rows, c, :].bitcast(F32),
                                            ALU.subtract).then_inc(ql_done, 1)

                for m in range(STEPS):
                    c, q, _ = place(m)
                    if c < CQ - 1:
                        low_13(b, c + 1, q)
                    if m:
                        low_h(m - 1)
                    if q == 0 and c:
                        low_q(c - 1)
                    if m == 5:
                        inv_std(NB + b - 1)
                low_h(STEPS - 1)
                low_q(CQ - 1)
                if not last:
                    for i in range(4):
                        low_13(b + 1, 0, i)

            for i in range(4):
                low_13(0, 0, i)
            steps_2(0, False)
            with pool.Fori(1, NB - 1) as b:
                steps_2(b, False)
            steps_2(NB - 1, True)
            inv_std(2 * NB - 1, FRONT)
            inv_std(2 * NB, BACK)

        @block.scalar
        def _(act):
            st = Steps(act, act_s)

            def high(count, slot, hi, piece):
                act.wait_ge(raw_in[slot], count)
                nc.scalar.copy(hi, piece).then_inc(hi_done, 1)

            def high_gu_piece(count, i):
                s = slice((i % 4) * 2 * CW, (i % 4 + 1) * 2 * CW)
                high(count, i % 4, wh[:, s], w_in_place[:, s])

            def high_d(base, d):
                rows = rows_in(NC - 1 - d // 2)
                s = slice((d % 4) * 512, (d % 4 + 1) * 512)
                high(landed(base, d), d % 4, wh[0:rows, s], w_in_place[0:rows, s])

            def head(b, base, i):
                for k in (2 * i, 2 * i + 1):
                    act.wait_ge(x_raw[k], 16 * b + 16)
                    nc.scalar.copy(xTh[:, k, :], x_in_place[:, k, :]).then_inc(x_hi, 1)
                high_gu_piece(landed(base, i), i)

            def evac(b, j, p, base):
                for t in range(NT):
                    if t < NT - 1:
                        act.wait_ge(g_done, 3 * NJ * b + 3 * j + t + 1)
                    else:
                        act.wait_ge(pe_used, base + 4 * j + 4)
                    if isinstance(b, int) and b == 0:
                        dst = s0[:, bass.ds(j, 1), t, :].rearrange("p o n -> p (o n)")
                    else:
                        dst = v[:, t, bass.ds(j * CW, CW)]
                    nc.scalar.activation(dst, banks[4 * p + t][:, 0:CW], ACT.Silu)\
                        .then_inc(g_freed, 1)

            def gate(b, base, first):
                def ahead(jj, pieces):
                    for i in pieces:
                        high_gu_piece(landed(base + 8 * jj, i), i)

                ahead(0, (4, 5))
                if not first:
                    turned(b - 1, NJ - 1, 1)
                ahead(0, (6, 7))
                evac(b, 0, 0, base)
                ahead(0, range(8, 12))
                evac(b, 1, 1, base)
                with act.Fori(1, NJ // 2 - 1) as jj:
                    for q in range(2):
                        ahead(jj, range(4 * q + 4, 4 * q + 8))
                        evac(b, 2 * jj + q, q, base)
                ahead(NJ // 2 - 1, range(4, 8))
                evac(b, NJ - 2, 0, base)

            def search(b, piece, fourth=True):
                for r in range(ROUNDS):
                    act.wait_ge(probe, ROUNDS * b + r + 1)
                    for t in (2, 3):
                        for h in range(2):
                            st.done()
                            ins = nc.scalar.activation(junka[:, :], v[:, t, h * (I // 2):(h + 1) * (I // 2)], ACT.Sign,
                                                       bias=negt[:, t:t + 1], accum_out=ssum[:, t - 2, h:h + 1])
                            st.mark(ins)
                            if t == 2 or h == 0:
                                piece()
                    st.done()
                    act.sem_inc(signs, 1)
                    if fourth:
                        piece()

            def turned(b, j, p):
                for m, c in enumerate(SETS[j]):
                    act.wait_ge(t_done, NC * b + c + 1)
                    if c == YC and not (isinstance(b, int) and b == 0):
                        act.wait_ge(x1_out, 16 * NT * b)
                    rows = rows_in(c)
                    nc.scalar.copy(hTh[0:rows, c, :], banks[4 * p + m][0:rows, :]).then_inc(t_hi, 1)

            def up(b, base, given, behind, other=None):
                for i in range(given, 4):
                    high_gu_piece(landed(base, i), i)
                for j in range(NJ):
                    for i in range(4):
                        if i == 2 and j:
                            turned(b, j - 1, (j - 1) % 2)
                        n = 4 * (j + 1) + i
                        if j == NJ - 1:
                            behind(i)
                        elif n >= given:
                            high_gu_piece(landed(base, n), n)
                    if j == 2 and other is not None:
                        other()

            def norm(b1, n, dst, sent):
                act.wait_ge(nb_ready, n + 1)
                for t in range(NT):
                    norm_tile(t)
                for t in range(NT):
                    send_tile(n, t, b1, dst, sent)

            def norm_tile(t):
                nc.scalar.activation(y[:, t, :], y[:, t, :], ACT.Identity, scale=rstd[:, t:t + 1],
                                     bias=nbias[:, t:t + 1]).then_inc(norm_done, 1)

            def send_tile(n, t, b1, dst, sent):
                act.wait_ge(norm_done, NT * n + t + 1)
                act.dma_start(dst[bass.ds(b1, 1), :, t, :].rearrange("o p h -> (o p) h"), y[:, t, :])\
                    .then_inc(sent, 16)

            for i in range(4):
                head(0, 0, i)
            gate(0, 0, True)
            for i in range(4):
                high_gu_piece(landed(NG, i), i)
            evac(0, NJ - 1, 1, 0)
            def copy_u(j, t):
                if t < NT - 1:
                    act.wait_ge(u_done, 3 * j + t + 1)
                else:
                    act.wait_ge(pe_used, NG + 4 * j + 4)
                nc.scalar.copy(w0[:, j, t, :], banks[4 * (j % 2) + t][:, 0:CW]).then_inc(u0_copied, 1)

            work = [(None, i) for i in range(4, 8)] + [(n // 4, n + 8) for n in range(NU)]

            def work_on_u():
                if work:
                    j, n = work.pop(0)
                    if j is not None:
                        copy_u(j, n % 4)
                    if n < NU:
                        high_gu_piece(landed(NG, n), n)

            search(0, work_on_u, False)
            while work:
                work_on_u()
            for i in range(4):
                head(1, USED0, i)
                turned(0, i, i % 2)
            for j in range(4, NJ - 1):
                turned(0, j, j % 2)

            def block_1(b, behind):
                base = used_base(b, False)
                gate(b, base, False)
                for d in range(4):
                    high_d(base + NG, d)
                evac(b, NJ - 1, 1, base)
                ahead_d = list(range(4, ND))
                search(b, lambda: high_d(base + NG, ahead_d.pop(0)))
                for d in ahead_d:
                    high_d(base + NG, d)
                up(b, base + NG + ND, 0, behind, lambda: norm(b - 1, b - 1, x1, x1_out))

            with act.Fori(1, NB - 1) as b:
                st.loop(b - 1, 4 * ROUNDS)
                block_1(b, lambda i: head(b + 1, used_base(b + 1, False), i))
                st.end(4 * ROUNDS, NB - 2)
            last_d = used_base(NB, False)
            block_1(NB - 1, lambda i: high_d(last_d, i) if i < 3 else None)
            turned(NB - 1, NJ - 1, 1)
            for d in range(3, ND):
                high_d(last_d, d)
                if d == 29:
                    act.wait_ge(b_in, 16 * 12)
                    nc.scalar.mul(b13[0:LR, :], braw[0:LR, 0:IB], LORA).then_inc(b_ready, 1)
                    nc.scalar.mul(b2s[0:LR, :], braw[0:LR, IB:IB + H], LORA).then_inc(b_ready, 1)
                if d >= ND - NW2 - 2 and d < ND - 2:
                    e = d - (ND - NW2 - 2)
                    if e == 0:
                        act.wait_ge(t_done, NC * NB)
                    c, sl, rows = e // 2, slice((e % 2) * 512, (e % 2 + 1) * 512), rows_of(e // 2)
                    act.wait_ge(w2_raw[e], 16)
                    nc.scalar.copy(w2h[0:rows, c, sl], w2_in_place[0:rows, c, sl]).then_inc(w2_hi, 1)

            def high_13(b, c, i):
                s, m = (c % 2) * 4 + i, steps_of(c) * rows_of(c)
                high(4 * (USED2 + NW13 * b) + 16 * (c + 1), i, w13h[:, s, 0:m], w13_in_place[:, s, 0:m])

            def turned_x(b, t):
                act.wait_ge(x1t_done, NT * b + t + 1)
                if not (isinstance(b, int) and b == 0 and t == 0):
                    act.wait_ge(t1_done, NT * b + t)
                    act.wait_ge(l_fold, NT * b + t)
                for i in range(2):
                    nc.scalar.copy(x1T[:, 4 * i:4 * i + 4, :].rearrange("p k t -> p (k t)"), banks[5 + i][:, :])\
                        .then_inc(x1t_ready, 1)

            def steps_2(b, before):
                def high_h(m):
                    rows = place(m)[2]
                    act.wait_ge(h_done, STEPS * b + m + 1)
                    if m >= 2:
                        act.wait_ge(t2_done, STEPS * b + m - 1)
                    nc.scalar.copy(h2h[0:rows, m % 2, :], h2[0:rows, m % 2, :]).then_inc(hh_done, 1)

                def high_q(c):
                    rows = rows_of(c)
                    act.wait_ge(f_done, CQ * b + c + 1)
                    nc.scalar.copy(hqh[0:rows, c, :], fold[0:rows, :]).then_inc(qh_done, 1)

                for m in range(STEPS):
                    c, q, rows = place(m)
                    if c < CQ - 1:
                        high_13(b, c + 1, q)
                    act.wait_ge(gg_done, STEPS * b + m + 1)
                    if m >= 2:
                        act.wait_ge(h_done, STEPS * b + m - 1)
                    nc.scalar.activation(sg[0:rows, m % 2, :], banks[2 * (m % 2)][0:rows, :], ACT.Silu).then_inc(s_done, 1)
                    if m:
                        high_h(m - 1)
                    if q == 0 and c:
                        high_q(c - 1)
                    t = (m - 8) // 2
                    if m == 8:
                        act.wait_ge(nb_ready, NB + b)
                    if 0 <= t < NT and m % 2 == 0:
                        norm_tile(t)
                    elif 0 <= t < NT:
                        send_tile(NB + b - 1, t, *before)
                high_h(STEPS - 1)
                high_q(CQ - 1)

            for i in range(4):
                high_13(0, 0, i)
            for t in range(NT):
                turned_x(0, t)
            def ready_for(b):
                for t in range(NT):
                    turned_x(b, t)
                    if t < 2:
                        high_13(b, 0, 2 * t)
                        high_13(b, 0, 2 * t + 1)

            steps_2(0, (NB - 1, x1, x1_out))
            ready_for(1)
            with act.Fori(1, NB - 1) as b:
                steps_2(b, (b - 1, out, out_done))
                ready_for(b + 1)
            steps_2(NB - 1, (NB - 2, out, out_done))
            for n, tiles in ((2 * NB - 1, range(NT - 1)), (2 * NB, (NT - 1,))):
                act.wait_ge(nb_ready, n + 1)
                for t in tiles:
                    norm_tile(t)
                    send_tile(2 * NB - 1, t, NB - 1, out, out_done)

        @block.vector
        def _(dve):
            st = Steps(dve, dve_s)
            es = Steps(dve, exact_s)
            EXACT = 2 + 31 * (5 + NT) + NT + 1 + NT * (1 + 7 * NJ)
            V = nc.vector
            dve.sem_inc(g_freed, 8)
            dve.sem_inc(u_freed, 8)
            dve.wait_ge(consts, 2)

            def step(ins):
                st.mark(ins)

            def take_gate_0():
                with dve.Fori(0, NJ) as j:
                    st.loop(j, NT)
                    for t in range(NT):
                        dve.wait_ge(g_freed, 8 + 4 * j + t + 1)
                        s = s0[:, bass.ds(j, 1), t, :].rearrange("p o n -> p (o n)")
                        step(V.scalar_tensor_tensor(out=v[:, t, bass.ds(j * CW, CW)], in0=s, scalar=-1.0, in1=s,
                                                    op0=ALU.mult, op1=ALU.max, accum_out=mags[:, t, bass.ds(j, 1)]))
                    st.end(NT, NJ)

            def take_gate(b):
                with dve.Fori(0, NJ // 2) as jj:
                    st.loop(jj, 16)
                    for q in range(2):
                        for t in range(NT):
                            dve.wait_ge(g_freed, 8 + 4 * NJ * b + 8 * jj + 4 * q + t + 1)
                            s = v[:, t, bass.ds((2 * jj + q) * CW, CW)]
                            step(V.tensor_scalar(sgn[:, t, bass.ds((2 * jj + q) * CW, CW)], s, 0.0, 2.0,
                                                 ALU.is_ge, ALU.mult))
                            st.done()
                            step(V.scalar_tensor_tensor(out=s, in0=s, scalar=-1.0, in1=s, op0=ALU.mult, op1=ALU.max,
                                                        accum_out=mags[:, t, bass.ds(2 * jj + q, 1)]))
                    st.end(16, NJ // 2)

            def say_probe():
                st.done()
                V.tensor_scalar(negt[:], tc[:, 0, :], -1.0, None, ALU.mult).then_inc(probe, 1)

            def count(b, r):
                say_probe()
                for t in (0, 1):
                    step(V.tensor_scalar(junkd[:, :], v[:, t, :], tc[:, 0, t:t + 1], None, ALU.is_lt, ALU.add,
                                         accum_out=tc[:, 1, t:t + 1]))
                    st.done()
                dve.wait_ge(signs, ROUNDS * b + r + 1)
                step(V.tensor_tensor(sadd[:], ssum[:, :, 0], ssum[:, :, 1], ALU.add))
                st.done()
                step(V.tensor_scalar(sadd[:], sadd[:], -0.5, I / 2 - 0.25, ALU.mult, ALU.add))
                st.done()
                step(V.tensor_scalar(tc[:, 1, 2:4], sadd[:], 12582912.0, -12582912.0, ALU.add, ALU.add))
                st.done()

            def search(b):
                st.done()
                step(V.tensor_reduce(le[:, 0, :], mags[:], AX.X, ALU.add))
                st.done()
                step(V.tensor_scalar(tc[:, 0, :], le[:, 0, :], 0.75 / I, None, ALU.mult))
                step(V.memset(lc[:], 0.0))
                step(V.tensor_scalar(hc[:, 0, :], le[:, 0, :], 2.001 / I, None, ALU.mult))
                step(V.memset(hc[:, 1, :], float(I)))
                for r in range(ROUNDS):
                    count(b, r)
                    step(V.tensor_scalar(le[:], tc[:, 1:2, :].broadcast_to((P, 2, NT)), KEEP_FROM + 0.5, None, ALU.is_le))
                    st.done()
                    step(V.scalar_tensor_tensor(out=qa[:], in0=le[:], scalar=BIG, in1=tc[:], op0=ALU.mult, op1=ALU.max))
                    step(V.scalar_tensor_tensor(out=qb[:], in0=le[:], scalar=BIG, in1=tc[:], op0=ALU.mult, op1=ALU.min))
                    st.done()
                    step(V.tensor_tensor(hc[:], hc[:], qa[:], ALU.min))
                    step(V.tensor_tensor(lc[:], lc[:], qb[:], ALU.max))
                    st.done()
                    if r == ROUNDS - 1:
                        break
                    step(V.tensor_tensor(qa[:], hc[:], lc[:], ALU.subtract))
                    step(V.tensor_scalar(qb[:, 0, :], lc[:, 1, :], -1.0, KEEP_FROM + 4.0, ALU.mult, ALU.add))
                    st.done()
                    step(V.reciprocal(qb[:, 1, :], qa[:, 1, :]))
                    step(V.tensor_tensor(qa[:, 0, :], qa[:, 0, :], qb[:, 0, :], ALU.mult))
                    st.done()
                    step(V.tensor_tensor(qa[:, 0, :], qa[:, 0, :], qb[:, 1, :], ALU.mult))
                    st.done()
                    step(V.tensor_tensor(tc[:, 0, :], qa[:, 0, :], lc[:, 0, :], ALU.add))
                step(V.tensor_scalar(qa[:, 0, :], hc[:, 1, :], -(KEEP_FROM + 1.0), None, ALU.add))
                Q = I // 2
                for t in range(NT):
                    for c in range(2):
                        st.done()
                        step(V.scalar_tensor_tensor(out=scr[:], in0=v[:, t, c * Q:(c + 1) * Q], scalar=hc[:, 0, t:t + 1],
                                                    in1=v[:, t, c * Q:(c + 1) * Q], op0=ALU.is_lt, op1=ALU.mult))
                        st.done_apart(passed_dve)
                        step(V.max(out=cand[:, 8 * c:8 * c + 8], in_=scr[:]))
                    st.done_apart(passed_dve)
                    step(V.max(out=top8[:], in_=cand[:]))
                    st.done()
                    step(V.scalar_tensor_tensor(out=pick[:], in0=iota8[:], scalar=qa[:, 0, t:t + 1], in1=top8[:],
                                                op0=ALU.is_equal, op1=ALU.mult, accum_out=tc[:, 0, t:t + 1]))
                    st.done()
                    step(V.tensor_scalar(junkd[:, :], v[:, t, :], tc[:, 0, t:t + 1], None, ALU.is_lt, ALU.add,
                                         accum_out=tc[:, 1, t:t + 1]))
                st.done()
                step(V.tensor_scalar(le[:, 0, :], tc[:, 1, :], float(KEEP_FROM), None, ALU.not_equal))
                st.done()
                V.tensor_reduce(bad[:], le[:, 0, :], AX.X, ALU.max).then_inc(bad_ready, 1)
                dve.wait_ge(flag_ready, b + 1)
                dve.sem_inc(passed_dve, 1)
                flagged = dve.value_load(flag[0:1, 0:1].bitcast(I32))
                with dve.If(flagged != 0):
                    exact()
                with dve.Else():
                    dve.sem_inc(exact_s, EXACT)

            def exact():
                found, trial = tc[:, 0, :].bitcast(I32), le[:, 0, :].bitcast(I32)
                es.mark(V.memset(found, 0))
                es.mark(V.memset(bit[:], 1 << 30))
                with dve.Fori(0, 31) as i:
                    es.loop(i, 5 + NT)
                    es.done()
                    es.mark(V.tensor_tensor(trial, found, bit[:], ALU.bitwise_or))
                    es.done()
                    for t in range(NT):
                        es.mark(V.tensor_scalar(junkd[:, :], v[:, t, :], le[:, 0, t:t + 1], None, ALU.is_lt, ALU.add,
                                                accum_out=tc[:, 1, t:t + 1]))
                        es.done()
                    es.mark(V.tensor_scalar(taken[:], tc[:, 1, :], KEEP_FROM - 0.5, None, ALU.is_lt))
                    es.done()
                    es.mark(V.tensor_tensor(taken[:], taken[:], bit[:], ALU.mult))
                    es.done()
                    es.mark(V.tensor_tensor(found, found, taken[:], ALU.bitwise_or))
                    es.mark(V.tensor_scalar(bit[:], bit[:], 1, None, ALU.logical_shift_right))
                    es.end(5 + NT, 31)
                es.done()
                for t in range(NT):
                    es.mark(V.tensor_scalar(junkd[:, :], v[:, t, :], tc[:, 0, t:t + 1], None, ALU.is_lt, ALU.add,
                                            accum_out=tc[:, 1, t:t + 1]))
                    es.done()
                es.mark(V.tensor_scalar(qa[:, 0, :], tc[:, 1, :], -1.0, float(KEEP_FROM), ALU.mult, ALU.add))
                eq, nth = scr[:, 0:CW], scr[:, CW:2 * CW]
                for t in range(NT):
                    es.mark(V.memset(carry[:], 0.0))
                    with dve.Fori(0, NJ) as j:
                        es.loop(j, 7)
                        es.done()
                        s = v[:, t, bass.ds(j * CW, CW)]
                        es.mark(V.tensor_scalar(eq, s, tc[:, 0, t:t + 1], None, ALU.is_equal))
                        es.done()
                        es.mark(V.tensor_tensor_scan(nth, eq, eq, carry[:, 0:1], ALU.add, ALU.max))
                        es.done()
                        es.mark(V.tensor_copy(carry[:], nth[:, CW - 1:CW]))
                        es.mark(V.scalar_tensor_tensor(out=eq, in0=nth, scalar=qa[:, 0, t:t + 1], in1=eq, op0=ALU.is_le,
                                                       op1=ALU.mult))
                        es.done()
                        es.mark(V.tensor_scalar(eq, eq, -1.0, 1.0, ALU.mult, ALU.add))
                        es.done()
                        es.mark(V.tensor_tensor(s, s, eq, ALU.mult))
                        es.done()
                        es.mark(V.scalar_tensor_tensor(out=s, in0=eq, scalar=-1.0, in1=s, op0=ALU.add, op1=ALU.add))
                        es.end(7, NJ)
                es.done_apart(passed_dve)
                assert es.n == EXACT

            def take_down(b1, used):
                dve.wait_ge(x_in, 16 * (b1 + 1))
                for n in range(2):
                    for t in range(NT):
                        if t < NT - 1:
                            dve.wait_ge(d_done, 6 * b1 + 3 * n + t + 1)
                        else:
                            dve.wait_ge(pe_used, used + ND - 1 + n)
                        s = y[:, t, n * 512:(n + 1) * 512]
                        V.tensor_tensor(s, banks[2 * t + n][:, :], s, ALU.add).then_inc(d_evac, 1)
                dve.wait_ge(d_evac, 8 * (b1 + 1))

            def norm_sums(n, tiles=range(NT), whole=slice(0, NT)):
                for t in tiles:
                    for i in range(2):
                        step(V.bn_stats(stats[:, t, i, :], y[:, t, i * 512:(i + 1) * 512]))
                    st.done_apart(passed_dve)
                    step(V.bn_aggr(mv[:, t, :], stats[:, t, :, :].rearrange("p n s -> p (n s)")))
                if tiles[-1] == whole.stop - 1:
                    st.done()
                    V.tensor_scalar(ve[:, whole], mv[:, whole, 1], EPS, None, ALU.add).then_inc(ve_ready, 1)

            def norm_bias(n, whole=slice(0, NT)):
                dve.wait_ge(rstd_ready, n + 1)
                V.scalar_tensor_tensor(out=nbias[:, whole], in0=mv[:, whole, 0], scalar=-1.0, in1=rstd[:, whole], op0=ALU.mult,
                                       op1=ALU.mult).then_inc(nb_ready, 1)

            def masked(b, j):
                for t in range(NT):
                    s, g = v[:, t, j * CW:(j + 1) * CW], sgn[:, t, j * CW:(j + 1) * CW]
                    st.done()
                    step(V.scalar_tensor_tensor(out=s, in0=s, scalar=tc[:, 0, t:t + 1], in1=s, op0=ALU.is_ge,
                                                op1=ALU.mult))
                    st.done()
                    step(V.scalar_tensor_tensor(out=s, in0=g, scalar=-1.0, in1=s, op0=ALU.add, op1=ALU.mult))

            def take_up(b, used, bias=None):
                masked(b, 0)
                for j in range(NJ):
                    for t in range(NT):
                        s = v[:, t, j * CW:(j + 1) * CW]
                        st.done()
                        if t < NT - 1:
                            dve.wait_ge(u_done, 3 * NJ * b + 3 * j + t + 1)
                        else:
                            dve.wait_ge(pe_used, used + 4 * j + 4)
                        V.tensor_tensor(s, banks[4 * (j % 2) + t][:, 0:CW], s, ALU.mult).then_inc(u_freed, 1)
                    if j < NJ - 1:
                        masked(b, j + 1)
                    if j == 1 and bias is not None:
                        norm_bias(bias)
                    turned(b, j)

            def turned(b, j):
                for m, c in enumerate(SETS[j]):
                    rows = rows_in(c)
                    dve.wait_ge(t_hi, NC * b + c + 1)
                    V.tensor_tensor(hTl[0:rows, c, :], banks[4 * (j % 2) + m][0:rows, :],
                                    hTh[0:rows, c, :].bitcast(F32), ALU.subtract).then_inc(t_lo, 1)

            def take_w0():
                for j in range(NJ):
                    for t in range(NT):
                        s = v[:, t, j * CW:(j + 1) * CW]
                        dve.wait_ge(w0_ready, 4 * j + t + 1)
                        V.scalar_tensor_tensor(out=s, in0=s, scalar=tc[:, 0, t:t + 1], in1=w0[:, j, t, :],
                                               op0=ALU.is_ge, op1=ALU.mult).then_inc(u_freed, 1)
                    if j:
                        turned(0, j - 1)
                turned(0, NJ - 1)

            take_gate_0()
            n0 = st.n
            search(0)
            es.base, es.n = EXACT, 0
            per = 2 * NT * NJ + (st.n - n0) + 3 * NT + 2 * NT * NJ
            take_w0()
            with dve.Fori(1, NB) as b:
                st.loop(b - 1, per)
                es.loop(b - 1, EXACT)
                take_gate(b)
                search(b)
                es.end(EXACT, NB - 1)
                used = used_base(b, False)
                take_down(b - 1, used + NG)
                norm_sums(b - 1)
                take_up(b, used + NG + ND, b - 1)
                st.end(per, NB - 1)
            dve.wait_ge(small_in, 16 * 2)
            step(V.tensor_copy(a2s[:, :, 0:R], a2raw[:, :, :]))
            st.done()
            V.tensor_tensor(a2s[:, :, R:2 * R], a2raw[:, :, :], a2s[:, :, 0:R].bitcast(F32), ALU.subtract)\
                .then_inc(a_ready, 1)
            dve.wait_ge(b_ready, 2)
            V.scalar_tensor_tensor(out=b13[64:LR, :], in0=braw[64:LR, 0:IB], scalar=LORA,
                                   in1=b13[64:LR, :].bitcast(F32), op0=ALU.mult, op1=ALU.subtract).then_inc(b_ready, 1)
            V.scalar_tensor_tensor(out=b2s[64:LR, :], in0=braw[64:LR, IB:IB + H], scalar=LORA,
                                   in1=b2s[64:LR, :].bitcast(F32), op0=ALU.mult, op1=ALU.subtract).then_inc(b_ready, 1)
            take_down(NB - 1, LAST_D)

            def fold_x(b, t):
                dve.wait_ge(x1t_ready, 2 * (NT * b + t + 1))
                if t == 0 and not (isinstance(b, int) and b == 0):
                    dve.wait_ge(uu_done, STEPS * b)
                st.done()
                V.tensor_reduce(xf[:], x1T[:, :, :].rearrange("p (q h) t -> p h t q", q=Q4), AX.X, ALU.add)\
                    .then_inc(l_fold, 1)
                dve.wait_ge(l_fold, NT * b + t + 1)
                tt = slice(t * P, (t + 1) * P)
                step(V.tensor_copy(xsh[:, :, tt], xf[:]))
                st.done()
                step(V.tensor_tensor(xsl[:, :, tt], xf[:], xsh[:, :, tt].bitcast(F32), ALU.subtract))

            def low_rank_x(b):
                dve.wait_ge(t1_done, NT * (b + 1))
                n = 2 * R
                step(V.tensor_copy(th[0:n, :], banks[7][0:n, :]))
                st.done()
                step(V.tensor_tensor(tl[0:n, :], banks[7][0:n, :], th[0:n, :].bitcast(F32), ALU.subtract))
                st.done()
                for i, dst in enumerate((lg, lu)):
                    for p0, src in ((0, th), (32, tl), (64, th)):
                        step(V.tensor_scalar(dst[p0:p0 + n, :], src[0:n, :].bitcast(F32), keep[0:n, i:i + 1], None,
                                             ALU.mult))
                st.done()
                dve.sem_inc(l_ready, 1)

            def steps_2(b):
                for m in range(STEPS):
                    c, q, rows = place(m)
                    dve.wait_ge(uu_done, STEPS * b + m + 1)
                    dve.wait_ge(s_done, STEPS * b + m + 1)
                    if m >= 2:
                        dve.wait_ge(hl_done, STEPS * b + m - 1)
                    st.done()
                    V.tensor_tensor(h2[0:rows, m % 2, :], banks[2 * (m % 2) + 1][0:rows, :], sg[0:rows, m % 2, :],
                                    ALU.mult).then_inc(h_done, 1)
                    dve.wait_ge(h_done, STEPS * b + m + 1)
                    last = q == steps_of(c) - 1
                    ins = None
                    if q == 1:
                        if c:
                            dve.wait_ge(ql_done, CQ * b + c)
                        ins = V.tensor_tensor(fold[0:rows, :], h2[0:rows, 0, :], h2[0:rows, 1, :], ALU.add)
                    elif q > 1:
                        st.done()
                        ins = V.tensor_tensor(fold[0:rows, :], fold[0:rows, :], h2[0:rows, m % 2, :], ALU.add)
                    if last:
                        ins.then_inc(f_done, 1)
                        dve.wait_ge(f_done, CQ * b + c + 1)
                    elif ins is not None:
                        step(ins)
                    if 1 <= m <= NT:
                        norm_sums(NB + b - 1, [m - 1])
                    if m == 7:
                        norm_bias(NB + b - 1)

            def low_rank_h(b):
                n = 2 * R
                dve.wait_ge(t2_done, STEPS * (b + 1))
                step(V.tensor_copy(t2s[0:n, :], banks[4][0:n, :]))
                step(V.tensor_copy(t2s[64:64 + n, :], banks[4][0:n, :]))
                st.done()
                V.tensor_tensor(t2s[32:32 + n, :], banks[4][0:n, :], t2s[0:n, :].bitcast(F32), ALU.subtract)\
                    .then_inc(t2_ready, 1)

            def take_out(b, t):
                if t == 0:
                    dve.wait_ge(y_in, 16 * (b + 1))
                for n in range(2):
                    dve.wait_ge(e_done, 2 * NT * b + 2 * t + n + 1)
                    s = y[:, t, n * 512:(n + 1) * 512]
                    V.tensor_tensor(s, banks[2 * (t % 2) + n][:, :], s, ALU.add).then_inc(e_evac, 1)

            dve.wait_ge(keep_ready, 5)
            for t in range(NT):
                fold_x(0, t)
            low_rank_x(0)
            def block_2(b):
                steps_2(b)
                low_rank_h(b)
                for t in range(NT):
                    fold_x(b + 1, t)
                    if t == NT - 1:
                        low_rank_x(b + 1)
                    take_out(b, t)
                dve.wait_ge(e_evac, 2 * NT * (b + 1))

            n0 = st.n
            block_2(0)
            per = st.n - n0
            with dve.Fori(1, NB - 1) as b:
                st.loop(b - 1, per)
                block_2(b)
                st.end(per, NB - 2)
            steps_2(NB - 1)
            low_rank_h(NB - 1)
            for t in range(NT):
                take_out(NB - 1, t)
                dve.wait_ge(e_evac, 2 * NT * (NB - 1) + 2 * (t + 1))
                norm_sums(2 * NB - 1 + t // (NT - 1), [t], FRONT if t < NT - 1 else BACK)
                if t == NT - 2:
                    norm_bias(2 * NB - 1, FRONT)
            norm_bias(2 * NB, BACK)

        @block.tensor
        def _(pe):
            pe.wait_ge(consts, 2)

            def three(dst, ah, al, bh, bl, start, stop):
                nc.tensor.matmul(dst, ah, bh, start=start, stop=False)
                nc.tensor.matmul(dst, ah, bl, start=False, stop=False)
                return nc.tensor.matmul(dst, al, bh, start=False, stop=stop)

            def chunk(b, base, jj, q, done, first_waits, inside=None, takes_x=False):
                for i in range(4):
                    pe.wait_ge(lo_done, base + 8 * jj + 4 * q + i + 1)
                    if takes_x:
                        pe.wait_ge(x_lo, KH * b + 2 * i + 2)
                    for k in (2 * i, 2 * i + 1):
                        w = slice(k * CW, (k + 1) * CW)
                        for t in range(NT):
                            if k == 0:
                                first_waits(t)
                            tt = slice(t * P, (t + 1) * P)
                            ins = three(banks[4 * q + t][:, 0:CW], xTh[:, k, tt], xTl[:, k, tt], wh[:, w],
                                        wl[:, w], k == 0, k == KH - 1)
                            if k == KH - 1 and t < NT - 1:
                                ins.then_inc(done, 1)
                    ins.then_inc(pe_used, 1)
                    if i == 2 and inside is not None:
                        inside()

            def turn(b, j, p):
                pe.wait_ge(u_freed, 8 + 4 * NJ * b + 4 * (j + 1))
                pe.sem_inc(passed_pe, 1)
                for m, c in enumerate(SETS[j]):
                    rows = rows_in(c)
                    for t in range(NT):
                        ins = nc.tensor.transpose(banks[4 * p + m][0:rows, t * P:(t + 1) * P],
                                                  v[:, t, c * P:c * P + rows], ident[:, :])
                    ins.then_inc(t_done, 1)

            def turned(b, j):
                pe.wait_ge(t_lo, NC * b + SETS[j][-1] + 1)
                pe.sem_inc(passed_pe, 1)

            def gate(b, base, first):
                def freed(j):
                    return lambda t: pe.wait_ge(g_freed, 4 * NJ * b + 4 * j + t + 1)
                if not first:
                    turned(b - 1, NJ - 2)
                chunk(b, base, 0, 0, g_done, freed(0), None if first else lambda: turn(b - 1, NJ - 1, 1), True)
                if not first:
                    turned(b - 1, NJ - 1)
                chunk(b, base, 0, 1, g_done, freed(1))
                with pe.Fori(1, NJ // 2) as jj:
                    for q in range(2):
                        chunk(b, base, jj, q, g_done, lambda t: pe.wait_ge(g_freed, 4 * NJ * b + 8 * jj + 4 * q + t + 1))

            def up(b, base, bank_waits):
                for j in range(NJ):
                    def waits(t):
                        if j < 2:
                            bank_waits(j, t)
                        pe.wait_ge(u_freed, 4 * NJ * b + 4 * j + t + 1)
                    if j >= 2:
                        turned(b, j - 2)
                    chunk(b, base, j // 2, j % 2, u_done, waits,
                          (lambda: turn(b, j - 1, (j - 1) % 2)) if j else None)

            def down(b1, base, bank_waits):
                for d in range(ND):
                    c, n = NC - 1 - d // 2, d % 2
                    rows = rows_in(c)
                    pe.wait_ge(lo_done, base + d + 1)
                    w = slice((d % 4) * 512, (d % 4 + 1) * 512)
                    for t in range(NT):
                        if d < 2 and t >= 2 or d == t == 0:
                            bank_waits(2 * t + n)
                        tt = slice(t * P, (t + 1) * P)
                        ins = three(banks[2 * t + n][:, :], hTh[0:rows, c, tt], hTl[0:rows, c, tt],
                                    wh[0:rows, w], wl[0:rows, w], d < 2, d >= ND - 2)
                        if d >= ND - 2 and t < NT - 1:
                            ins.then_inc(d_done, 1)
                    ins.then_inc(pe_used, 1)

            def silu_taken(b, n):
                pe.wait_ge(g_freed, 4 * NJ * (b + 1) + n)
                pe.sem_inc(passed_pe, 1)

            def copied(n):
                pe.wait_ge(u0_copied, n)

            gate(0, 0, True)
            for j in range(NJ):
                chunk(0, NG, j // 2, j % 2, u_done,
                      lambda t: silu_taken(0, 4 * j + t + 1) if j < 2 else copied(4 * (j - 2) + t + 1))
            for j in range(NJ - 1):
                if j < 2:
                    copied(4 * (NJ - 2 + j) + 4)
                else:
                    turned(0, j - 2)
                turn(0, j, j % 2)
            with pe.Fori(1, NB) as b:
                base = used_base(b, False)
                gate(b, base, False)
                down(b - 1, base + NG, lambda bank: silu_taken(b, max(bank + 1, 4)))

                def y_taken(j, t):
                    bank = 4 * j + t
                    pe.wait_ge(d_evac, 8 * (b - 1) + 4 * (bank % 2) + bank // 2 + 1)
                    pe.sem_inc(passed_pe, 1)

                up(b, base + NG + ND, y_taken)
            turn(NB - 1, NJ - 1, 1)
            turned(NB - 1, NJ - 1)
            down(NB - 1, used_base(NB, False), lambda bank: None)

            def turn_x(b, t):
                pe.wait_ge(xa_in[t % 2], 16 * (2 * b + t // 2 + 1))
                if not (isinstance(b, int) and b == 0 and t == 0):
                    pe.wait_ge(x1t_ready, 2 * (NT * b + t))
                for k in range(KH):
                    ins = nc.tensor.transpose(banks[5 + k // 4][:, (k % 4) * P:(k % 4 + 1) * P],
                                              xa[:, t % 2, k * P:(k + 1) * P], ident[:, :])
                ins.then_inc(x1t_done, 1)

            def low_rank(b, t):
                pe.wait_ge(x1t_ready, 2 * (NT * b + t + 1))
                pe.sem_inc(passed_pe, 1)
                for k in range(KH):
                    ins = nc.tensor.matmul(banks[7][0:2 * R, t * P:(t + 1) * P], a13s[:, k, :], x1T[:, k, :],
                                           start=k == 0, stop=k == KH - 1)
                ins.then_inc(t1_done, 1)

            def low_h(b, m, frees):
                c, q, rows = place(m)
                pe.wait_ge(hl_done, STEPS * b + m + 1)
                pe.sem_inc(passed_pe, 1)
                w = a2s[0:rows, m, :]
                i1 = nc.tensor.matmul(banks[4][0:2 * R, :], w, h2h[0:rows, m % 2, :], start=m == 0, stop=False)
                if frees:
                    i1.then_inc(pe_used, 4)
                nc.tensor.matmul(banks[4][0:2 * R, :], w, h2l[0:rows, m % 2, :], start=False,
                                 stop=m == STEPS - 1).then_inc(t2_done, 1)

            def steps_2(b):
                base = USED2 + NW13 * b
                pe.wait_ge(l_ready, b + 1)

                for m in range(STEPS):
                    c, q, rows = place(m)
                    if q == 0:
                        pe.wait_ge(lo_done, base + 4 * c + 4)
                        pe.sem_inc(passed_pe, 1)
                    if m < 2 and not (isinstance(b, int) and b == 0):
                        pe.wait_ge(e_evac, 2 * NT * b - 2 + 2 * m)
                        pe.sem_inc(passed_pe, 1)
                    for i, (low_x, done) in enumerate(((lg, gg_done), (lu, uu_done))):
                        dst = banks[2 * (m % 2) + i][0:rows, :]
                        if m >= 2:
                            pe.wait_ge((s_done, h_done)[i], STEPS * b + m - 1)
                            pe.sem_inc(passed_pe, 1)
                        for k in range(KQ):
                            s, mm = (c % 2) * 4 + 2 * i + k, slice(q * rows, (q + 1) * rows)
                            three(dst, w13h[:, s, mm], w13l[:, s, mm], xsh[:, k, :], xsl[:, k, :], k == 0, False)
                        mm = slice(c * Q4 * P + q * rows, c * Q4 * P + (q + 1) * rows)
                        nc.tensor.matmul(dst, b13[0:LR, mm], low_x[0:LR, :], start=False, stop=True).then_inc(done, 1)
                    if m >= 2:
                        low_h(b, m - 2, q == steps_of(c) - 1)
                low_h(b, STEPS - 2, False)

            def down_2(b, t, between=None):
                if t == 0:
                    pe.wait_ge(ql_done, CQ * b + CQ - 1)
                    pe.sem_inc(passed_pe, 1)
                elif t >= 2:
                    pe.wait_ge(e_evac, 2 * NT * b + 2 * (t - 1))
                    pe.sem_inc(passed_pe, 1)
                tt = slice(t * P, (t + 1) * P)
                for n in range(2):
                    w = slice(n * 512, (n + 1) * 512)
                    for c in range(CQ):
                        rows = rows_of(c)
                        if t == n == 0 and c == CQ - 1:
                            low_h(b, STEPS - 1, False)
                            pe.wait_ge(ql_done, CQ * (b + 1))
                            pe.sem_inc(passed_pe, 1)
                        three(banks[2 * (t % 2) + n][:, :], hqh[0:rows, c, tt], hql[0:rows, c, tt], w2h[0:rows, c, w],
                              w2l[0:rows, c, w], c == 0, False)
                    if n == 0 and between is not None:
                        between()
                if t == 0:
                    pe.wait_ge(t2_ready, b + 1)
                    pe.sem_inc(passed_pe, 1)
                for n in range(2):
                    nc.tensor.matmul(banks[2 * (t % 2) + n][:, :], t2s[0:LR, tt], b2s[0:LR, n * 512:(n + 1) * 512],
                                     start=False, stop=True).then_inc(e_done, 1)

            pe.wait_ge(small_in, 16 * 2)
            pe.wait_ge(d_evac, 8 * NB)
            for t in range(NT):
                turn_x(0, t)
                low_rank(0, t)
            pe.wait_ge(b_ready, 4)
            pe.wait_ge(a_ready, 1)
            pe.wait_ge(keep_ready, 5)
            pe.wait_ge(w2_lo, NW2)
            def block_2(b):
                steps_2(b)
                for t in range(NT):
                    turn_x(b + 1, t)
                    down_2(b, t, lambda: low_rank(b + 1, t))

            block_2(0)
            with pe.Fori(1, NB - 1) as b:
                block_2(b)
            steps_2(NB - 1)
            for t in range(NT):
                down_2(NB - 1, t)


def kernel(L0_attn_x, L0_attn_w_gate, L0_attn_w_up, L0_attn_w_down, L0_ffn_w1q, L0_ffn_a1, L0_ffn_b1, L0_ffn_w3q,
           L0_ffn_a3, L0_ffn_b3, L0_ffn_w2q, L0_ffn_a2, L0_ffn_b2):
    import numpy as np
    import concourse.bacc as bacc
    from concourse.bass_utils import run_bass_kernel_spmd as run

    x = np.asarray(L0_attn_x).reshape(TOK, H)
    def turned(a):
        return np.ascontiguousarray(np.asarray(a).T)

    xT = np.ascontiguousarray(x.reshape(NB, TB, KH, P).transpose(0, 3, 2, 1)).reshape(NB, P, KH * TB)
    xtok = np.ascontiguousarray(x.reshape(NB, NT, P, H).transpose(0, 2, 1, 3))

    def by_chunk(w):
        w = np.asarray(w).reshape(NJ, CW, KH, P)
        return np.ascontiguousarray(w.transpose(0, 3, 2, 1)).reshape(NJ, P, KH * CW)

    def by_step(a):
        rest = a.shape[1:]
        a = a.reshape(Q4, IQ, *rest)
        out = np.zeros((CQ, Q4, P, *rest), a.dtype)
        out[:CQ - 1] = a[:, :(CQ - 1) * P].reshape(Q4, CQ - 1, P, *rest).swapaxes(0, 1)
        flat = out[CQ - 1].reshape(Q4 * P, *rest)
        for q in range(Q4):
            at = q // 2 * PAIR + q % 2 * HALF
            flat[at:at + LASTQ] = a[q, (CQ - 1) * P:]
        return out.reshape(CQ, Q4 * P, *rest)

    w13 = np.stack([by_step(np.asarray(w).reshape(I, KQ, P)) for w in (L0_ffn_w1q, L0_ffn_w3q)])
    w13 = np.ascontiguousarray(w13.transpose(1, 0, 3, 4, 2))

    def low_b(b):
        return np.ascontiguousarray(by_step(np.asarray(b)).reshape(CQ * Q4 * P, R)[:IB].T)

    a2 = by_step(turned(L0_ffn_a2))
    a2p = np.zeros((P, STEPS, R), a2.dtype)
    for m in range(STEPS):
        c, q, rows = place(m)
        a2p[:rows, m] = a2[c, q * rows:(q + 1) * rows]
    w2 = np.zeros((CQ, P, H), a2.dtype)
    w2t = turned(L0_ffn_w2q)
    w2[:CQ - 1] = w2t[:(CQ - 1) * P].reshape(CQ - 1, P, H)
    for at in (0, HALF):
        w2[CQ - 1, at:at + LASTQ] = w2t[(CQ - 1) * P:]
    a13 = np.concatenate([np.asarray(L0_ffn_a1), np.asarray(L0_ffn_a3)]).reshape(2 * R, KH, P)

    arrays = {"in_xT": xT, "in_xtok": xtok, "in_wg": by_chunk(L0_attn_w_gate), "in_wu": by_chunk(L0_attn_w_up),
              "in_wd": turned(L0_attn_w_down), "in_w13": w13, "in_w2": w2,
              "in_a13": np.ascontiguousarray(a13.transpose(2, 1, 0)), "in_a2": a2p,
              "in_b1": low_b(L0_ffn_b1), "in_b3": low_b(L0_ffn_b3), "in_b2": turned(L0_ffn_b2)}
    nc = bacc.Bacc("TRN2", target_bir_lowering=False, num_devices=1)
    aps = [nc.dram_tensor(n, a.shape, F32, kind="ExternalInput").ap() for n, a in arrays.items()]
    o = nc.dram_tensor("out_y", (NB, P, NT, H), F32, kind="ExternalOutput").ap()
    program(nc, *aps, o)
    r = run(nc, [arrays], core_ids=[0])
    return np.ascontiguousarray(r.results[0]["out_y"].transpose(0, 2, 1, 3)).reshape(2, 1024, 1024)
```
